# Optimizing a Trainium2 kernel written in Bass

```python
import numpy as np
import jax
import jax.numpy as jnp

def _softmax(x, axis=-1):
    return jax.nn.softmax(x, axis=axis)

def _gelu(x):
    return jax.nn.gelu(x, approximate=True)

def _silu(x):
    return jax.nn.silu(x)

def _sigmoid(x):
    return jax.nn.sigmoid(x)

def _layernorm(x, axis=-1, eps=1e-05):
    m = jnp.mean(x, axis=axis, keepdims=True)
    v = jnp.var(x, axis=axis, keepdims=True)
    return (x - m) / jnp.sqrt(v + eps)

def _scatter_add(tgt, idx, src, axis=0):
    return tgt.at[idx].add(src)

def _segment_sum(src, seg, n):
    return jax.ops.segment_sum(src, seg, n)
kernel_name = 'mk_vit_tower_d1_tok_img768_r4_30b605'

def setup_inputs(seed: int=0):
    np.random.seed(seed)
    _w = jnp.asarray

    def _rec_inputs():
        import jax
        import jax.numpy as jnp
        _rk = jax.random.key(seed)
        x = -0.000596345 + 1.00056 * jax.random.normal(jax.random.fold_in(_rk, 1), (64, 3, 128, 128), jnp.float32)
        return x
    x = _rec_inputs()

    def _L0_tok_setup():
        import jax, jax.numpy as jnp
        import numpy as np
        IMG = 128
        P = 16
        ND = IMG // P
        N = ND * ND
        INF = 3 * P * P
        ATT = 192
        HID = 768
        OUT = 192
        B = 64
        EPS = 1e-05

        def _forward(x, Wq, bq, Wk, bk, Wv, bv, ln_g, ln_b, p1_w, p1_b, w0, b0, w1, b1, w2, b2, w3, b3, w4, b4, p2_w, p2_b):
            b_ = x.shape[0]
            flat = x.reshape(b_, 3, ND, P, ND, P).transpose(0, 2, 4, 1, 3, 5).reshape(b_, N, INF)
            q = jnp.einsum('bnf,nfd->bnd', flat, Wq) + bq
            k = jnp.einsum('bnf,nfd->bnd', flat, Wk) + bk
            v = jnp.einsum('bnf,nfd->bnd', flat, Wv) + bv
            scores = jnp.einsum('bnd,cnd->nbc', q, k) / jnp.sqrt(jnp.float32(ATT))
            attn = jnp.einsum('nbc,cnd->bnd', jax.nn.softmax(scores, axis=-1), v)
            mu = attn.mean(-1, keepdims=True)
            var = ((attn - mu) ** 2).mean(-1, keepdims=True)
            ln = (attn - mu) / jnp.sqrt(var + EPS) * ln_g + ln_b
            att = ln + flat @ p1_w + p1_b
            h = att @ w0 + b0
            h = h @ w1 + b1
            h = h @ w2 + b2
            h = h @ w3 + b3
            h = h @ w4 + b4
            proj = h + att @ p2_w + p2_b
            return jax.nn.softmax(proj, axis=2)
        key = jax.random.key(seed)
        ks = jax.random.split(key, 24)
        w = lambda k, shape: jax.random.normal(k, shape, jnp.float32) * 0.02
        return {'x': jax.random.normal(ks[0], (B, 3, IMG, IMG), jnp.float32), 'Wq': w(ks[1], (N, INF, ATT)), 'bq': w(ks[2], (N, ATT)), 'Wk': w(ks[3], (N, INF, ATT)), 'bk': w(ks[4], (N, ATT)), 'Wv': w(ks[5], (N, INF, ATT)), 'bv': w(ks[6], (N, ATT)), 'ln_g': jnp.ones((ATT,), jnp.float32), 'ln_b': jnp.zeros((ATT,), jnp.float32), 'p1_w': w(ks[7], (INF, ATT)), 'p1_b': w(ks[8], (ATT,)), 'w0': w(ks[9], (ATT, HID)), 'b0': w(ks[10], (HID,)), 'w1': w(ks[11], (HID, HID)), 'b1': w(ks[12], (HID,)), 'w2': w(ks[13], (HID, HID)), 'b2': w(ks[14], (HID,)), 'w3': w(ks[15], (HID, HID)), 'b3': w(ks[16], (HID,)), 'w4': w(ks[17], (HID, OUT)), 'b4': w(ks[18], (OUT,)), 'p2_w': w(ks[19], (ATT, OUT)), 'p2_b': w(ks[20], (OUT,))}
    _L0_tok_all = _L0_tok_setup()
    _L0_tok_in = {k: v for k, v in _L0_tok_all.items() if k in ('Wq', 'bq', 'Wk', 'bk', 'Wv', 'bv', 'ln_g', 'ln_b', 'p1_w', 'p1_b', 'w0', 'b0', 'w1', 'b1', 'w2', 'b2', 'w3', 'b3', 'w4', 'b4', 'p2_w', 'p2_b')}
    del _L0_tok_all

    def _L0_attn_setup():
        import jax, jax.numpy as jnp
        import numpy as np
        B, S, D, H, HD = (4, 512, 192, 12, 64)
        P = H * HD
        LR = 0.1

        def _ln(x, g, b, eps=1e-05):
            m = jnp.mean(x, axis=-1, keepdims=True)
            v = jnp.mean((x - m) ** 2, axis=-1, keepdims=True)
            return (x - m) / jnp.sqrt(v + eps) * g + b

        def _modifier(x, w1, b1, w2, b2):
            h = jax.nn.gelu(x @ w1.T + b1, approximate=False)
            return h @ w2.T + b2

        def _reference_tuple_inner(x, ln_in_g, ln_in_b, Wk, Wv, Wq, km_w1, km_b1, km_w2, km_b2, vm_w1, vm_b1, vm_w2, vm_b2, qm_w1, qm_b1, qm_w2, qm_b2, lnk_g, lnk_b, lnv_g, lnv_b, lnq_g, lnq_b, Wo, lr_scale, Wg, bg):
            b, s, d = x.shape
            xn = _ln(x, ln_in_g, ln_in_b)
            k = xn @ Wk.T + 0.1 * _modifier(xn, km_w1, km_b1, km_w2, km_b2)
            v = xn @ Wv.T + 0.1 * _modifier(xn, vm_w1, vm_b1, vm_w2, vm_b2)
            q = xn @ Wq.T + 0.1 * _modifier(xn, qm_w1, qm_b1, qm_w2, qm_b2)
            k = _ln(k.reshape(b, s, H, HD), lnk_g, lnk_b)
            v = _ln(v.reshape(b, s, H, HD), lnv_g, lnv_b)
            q = _ln(q.reshape(b, s, H, HD), lnq_g, lnq_b)
            k_s = jnp.transpose(k, (1, 0, 2, 3))
            v_s = jnp.transpose(v, (1, 0, 2, 3))
            q_s = jnp.transpose(q, (1, 0, 2, 3))
            lr = jax.nn.sigmoid(lr_scale) * LR * 2.0
            M0 = jnp.zeros((b, H, HD, HD), x.dtype)

            def step(M, kvq):
                k_t, v_t, q_t = kvq
                out_t = jnp.einsum('bhdk,bhk->bhd', M, q_t)
                kn = k_t / (jnp.linalg.norm(k_t, axis=-1, keepdims=True) + 1e-06)
                pred = jnp.einsum('bhdk,bhk->bhd', M, kn)
                surprise = pred - v_t
                coef = pred + lr[None, :, None] * surprise
                M_new = M - jnp.einsum('bhd,bhk->bhdk', coef, kn)
                return (M_new, out_t)
            M_final, outs = jax.lax.scan(step, M0, (k_s, v_s, q_s))
            out = jnp.transpose(outs, (1, 0, 2, 3)).reshape(b, s, H * HD)
            out = out @ Wo.T
            gate = jax.nn.sigmoid(x @ Wg.T + bg)
            out = gate * out
            return (out, M_final)
        key = jax.random.key(seed)
        ks = jax.random.split(key, 16)

        def n(k, shape, s=0.02):
            return jax.random.normal(k, shape, jnp.float32) * s
        inp = {}
        inp['x'] = jax.random.normal(ks[0], (B, S, D), jnp.float32)
        inp['ln_in_g'] = jnp.ones((D,), jnp.float32)
        inp['ln_in_b'] = jnp.zeros((D,), jnp.float32)
        inp['Wk'] = n(ks[1], (P, D))
        inp['Wv'] = n(ks[2], (P, D))
        inp['Wq'] = n(ks[3], (P, D))
        inp['km_w1'] = n(ks[4], (D // 4, D), 0.01)
        inp['km_b1'] = jnp.zeros((D // 4,), jnp.float32)
        inp['km_w2'] = n(ks[5], (P, D // 4), 0.01)
        inp['km_b2'] = jnp.zeros((P,), jnp.float32)
        inp['vm_w1'] = n(ks[6], (D // 4, D), 0.01)
        inp['vm_b1'] = jnp.zeros((D // 4,), jnp.float32)
        inp['vm_w2'] = n(ks[7], (P, D // 4), 0.01)
        inp['vm_b2'] = jnp.zeros((P,), jnp.float32)
        inp['qm_w1'] = n(ks[8], (D // 4, D), 0.01)
        inp['qm_b1'] = jnp.zeros((D // 4,), jnp.float32)
        inp['qm_w2'] = n(ks[9], (P, D // 4), 0.01)
        inp['qm_b2'] = jnp.zeros((P,), jnp.float32)
        inp['lnk_g'] = jnp.ones((HD,), jnp.float32)
        inp['lnk_b'] = jnp.zeros((HD,), jnp.float32)
        inp['lnv_g'] = jnp.ones((HD,), jnp.float32)
        inp['lnv_b'] = jnp.zeros((HD,), jnp.float32)
        inp['lnq_g'] = jnp.ones((HD,), jnp.float32)
        inp['lnq_b'] = jnp.zeros((HD,), jnp.float32)
        inp['Wo'] = n(ks[10], (D, P))
        inp['lr_scale'] = jnp.ones((H,), jnp.float32)
        inp['Wg'] = n(ks[11], (D, D))
        inp['bg'] = jnp.zeros((D,), jnp.float32)
        return inp
    _L0_attn_all = _L0_attn_setup()
    _L0_attn_in = {k: v for k, v in _L0_attn_all.items() if k in ('ln_in_g', 'ln_in_b', 'Wk', 'Wv', 'Wq', 'km_w1', 'km_b1', 'km_w2', 'km_b2', 'vm_w1', 'vm_b1', 'vm_w2', 'vm_b2', 'qm_w1', 'qm_b1', 'qm_w2', 'qm_b2', 'lnk_g', 'lnk_b', 'lnv_g', 'lnv_b', 'lnq_g', 'lnq_b', 'Wo', 'lr_scale', 'Wg', 'bg')}
    del _L0_attn_all

    def _L0_ffn_setup():
        import jax, jax.numpy as jnp
        import numpy as np
        HIDDEN = 192
        INNER = 128
        EPS = 1e-05
        key = jax.random.key(seed)
        ks = jax.random.split(key, 6)
        B, S = (8, 1024)
        x = jax.random.normal(ks[0], (B, S, HIDDEN), dtype=jnp.float32)
        W1 = jax.random.normal(ks[1], (INNER, HIDDEN), dtype=jnp.float32) * 0.02
        b1 = jnp.zeros((INNER,), dtype=jnp.float32)
        W2 = jax.random.normal(ks[2], (HIDDEN, INNER), dtype=jnp.float32) * 0.02
        b2 = jnp.zeros((HIDDEN,), dtype=jnp.float32)
        bound = 1.0 / np.sqrt(HIDDEN)
        Wo = jax.random.uniform(ks[3], (HIDDEN, HIDDEN), minval=-bound, maxval=bound, dtype=jnp.float32)
        bo = jax.random.uniform(ks[4], (HIDDEN,), minval=-bound, maxval=bound, dtype=jnp.float32)
        gamma = jnp.ones((HIDDEN,), dtype=jnp.float32)
        beta = jnp.zeros((HIDDEN,), dtype=jnp.float32)
        return {'x': x, 'W1': W1, 'b1': b1, 'W2': W2, 'b2': b2, 'Wo': Wo, 'bo': bo, 'gamma': gamma, 'beta': beta}
    _L0_ffn_all = _L0_ffn_setup()
    _L0_ffn_in = {k: v for k, v in _L0_ffn_all.items() if k in ('W1', 'b1', 'W2', 'b2', 'Wo', 'bo', 'gamma', 'beta')}
    del _L0_ffn_all
    return {'x': x, 'L0_tok_Wq': _L0_tok_in['Wq'], 'L0_tok_bq': _L0_tok_in['bq'], 'L0_tok_Wk': _L0_tok_in['Wk'], 'L0_tok_bk': _L0_tok_in['bk'], 'L0_tok_Wv': _L0_tok_in['Wv'], 'L0_tok_bv': _L0_tok_in['bv'], 'L0_tok_ln_g': _L0_tok_in['ln_g'], 'L0_tok_ln_b': _L0_tok_in['ln_b'], 'L0_tok_p1_w': _L0_tok_in['p1_w'], 'L0_tok_p1_b': _L0_tok_in['p1_b'], 'L0_tok_w0': _L0_tok_in['w0'], 'L0_tok_b0': _L0_tok_in['b0'], 'L0_tok_w1': _L0_tok_in['w1'], 'L0_tok_b1': _L0_tok_in['b1'], 'L0_tok_w2': _L0_tok_in['w2'], 'L0_tok_b2': _L0_tok_in['b2'], 'L0_tok_w3': _L0_tok_in['w3'], 'L0_tok_b3': _L0_tok_in['b3'], 'L0_tok_w4': _L0_tok_in['w4'], 'L0_tok_b4': _L0_tok_in['b4'], 'L0_tok_p2_w': _L0_tok_in['p2_w'], 'L0_tok_p2_b': _L0_tok_in['p2_b'], 'L0_attn_ln_in_g': _L0_attn_in['ln_in_g'], 'L0_attn_ln_in_b': _L0_attn_in['ln_in_b'], 'L0_attn_Wk': _L0_attn_in['Wk'], 'L0_attn_Wv': _L0_attn_in['Wv'], 'L0_attn_Wq': _L0_attn_in['Wq'], 'L0_attn_km_w1': _L0_attn_in['km_w1'], 'L0_attn_km_b1': _L0_attn_in['km_b1'], 'L0_attn_km_w2': _L0_attn_in['km_w2'], 'L0_attn_km_b2': _L0_attn_in['km_b2'], 'L0_attn_vm_w1': _L0_attn_in['vm_w1'], 'L0_attn_vm_b1': _L0_attn_in['vm_b1'], 'L0_attn_vm_w2': _L0_attn_in['vm_w2'], 'L0_attn_vm_b2': _L0_attn_in['vm_b2'], 'L0_attn_qm_w1': _L0_attn_in['qm_w1'], 'L0_attn_qm_b1': _L0_attn_in['qm_b1'], 'L0_attn_qm_w2': _L0_attn_in['qm_w2'], 'L0_attn_qm_b2': _L0_attn_in['qm_b2'], 'L0_attn_lnk_g': _L0_attn_in['lnk_g'], 'L0_attn_lnk_b': _L0_attn_in['lnk_b'], 'L0_attn_lnv_g': _L0_attn_in['lnv_g'], 'L0_attn_lnv_b': _L0_attn_in['lnv_b'], 'L0_attn_lnq_g': _L0_attn_in['lnq_g'], 'L0_attn_lnq_b': _L0_attn_in['lnq_b'], 'L0_attn_Wo': _L0_attn_in['Wo'], 'L0_attn_lr_scale': _L0_attn_in['lr_scale'], 'L0_attn_Wg': _L0_attn_in['Wg'], 'L0_attn_bg': _L0_attn_in['bg'], 'L0_ffn_W1': _L0_ffn_in['W1'], 'L0_ffn_b1': _L0_ffn_in['b1'], 'L0_ffn_W2': _L0_ffn_in['W2'], 'L0_ffn_b2': _L0_ffn_in['b2'], 'L0_ffn_Wo': _L0_ffn_in['Wo'], 'L0_ffn_bo': _L0_ffn_in['bo'], 'L0_ffn_gamma': _L0_ffn_in['gamma'], 'L0_ffn_beta': _L0_ffn_in['beta']}

def reference(x, L0_tok_Wq, L0_tok_bq, L0_tok_Wk, L0_tok_bk, L0_tok_Wv, L0_tok_bv, L0_tok_ln_g, L0_tok_ln_b, L0_tok_p1_w, L0_tok_p1_b, L0_tok_w0, L0_tok_b0, L0_tok_w1, L0_tok_b1, L0_tok_w2, L0_tok_b2, L0_tok_w3, L0_tok_b3, L0_tok_w4, L0_tok_b4, L0_tok_p2_w, L0_tok_p2_b, L0_attn_ln_in_g, L0_attn_ln_in_b, L0_attn_Wk, L0_attn_Wv, L0_attn_Wq, L0_attn_km_w1, L0_attn_km_b1, L0_attn_km_w2, L0_attn_km_b2, L0_attn_vm_w1, L0_attn_vm_b1, L0_attn_vm_w2, L0_attn_vm_b2, L0_attn_qm_w1, L0_attn_qm_b1, L0_attn_qm_w2, L0_attn_qm_b2, L0_attn_lnk_g, L0_attn_lnk_b, L0_attn_lnv_g, L0_attn_lnv_b, L0_attn_lnq_g, L0_attn_lnq_b, L0_attn_Wo, L0_attn_lr_scale, L0_attn_Wg, L0_attn_bg, L0_ffn_W1, L0_ffn_b1, L0_ffn_W2, L0_ffn_b2, L0_ffn_Wo, L0_ffn_bo, L0_ffn_gamma, L0_ffn_beta):
    import jax
    import jax.numpy as jnp

    def _L0_tok_ref(x, Wq, bq, Wk, bk, Wv, bv, ln_g, ln_b, p1_w, p1_b, w0, b0, w1, b1, w2, b2, w3, b3, w4, b4, p2_w, p2_b):
        import jax, jax.numpy as jnp
        import numpy as np
        IMG = 128
        P = 16
        ND = IMG // P
        N = ND * ND
        INF = 3 * P * P
        ATT = 192
        HID = 768
        OUT = 192
        B = 64
        EPS = 1e-05

        def _forward(x, Wq, bq, Wk, bk, Wv, bv, ln_g, ln_b, p1_w, p1_b, w0, b0, w1, b1, w2, b2, w3, b3, w4, b4, p2_w, p2_b):
            b_ = x.shape[0]
            flat = x.reshape(b_, 3, ND, P, ND, P).transpose(0, 2, 4, 1, 3, 5).reshape(b_, N, INF)
            q = jnp.einsum('bnf,nfd->bnd', flat, Wq) + bq
            k = jnp.einsum('bnf,nfd->bnd', flat, Wk) + bk
            v = jnp.einsum('bnf,nfd->bnd', flat, Wv) + bv
            scores = jnp.einsum('bnd,cnd->nbc', q, k) / jnp.sqrt(jnp.float32(ATT))
            attn = jnp.einsum('nbc,cnd->bnd', jax.nn.softmax(scores, axis=-1), v)
            mu = attn.mean(-1, keepdims=True)
            var = ((attn - mu) ** 2).mean(-1, keepdims=True)
            ln = (attn - mu) / jnp.sqrt(var + EPS) * ln_g + ln_b
            att = ln + flat @ p1_w + p1_b
            h = att @ w0 + b0
            h = h @ w1 + b1
            h = h @ w2 + b2
            h = h @ w3 + b3
            h = h @ w4 + b4
            proj = h + att @ p2_w + p2_b
            return jax.nn.softmax(proj, axis=2)
        return _forward(x, Wq, bq, Wk, bk, Wv, bv, ln_g, ln_b, p1_w, p1_b, w0, b0, w1, b1, w2, b2, w3, b3, w4, b4, p2_w, p2_b)

    def _L0_attn_ref(x, ln_in_g, ln_in_b, Wk, Wv, Wq, km_w1, km_b1, km_w2, km_b2, vm_w1, vm_b1, vm_w2, vm_b2, qm_w1, qm_b1, qm_w2, qm_b2, lnk_g, lnk_b, lnv_g, lnv_b, lnq_g, lnq_b, Wo, lr_scale, Wg, bg):
        import jax, jax.numpy as jnp
        import numpy as np
        B, S, D, H, HD = (4, 512, 192, 12, 64)
        P = H * HD
        LR = 0.1

        def _ln(x, g, b, eps=1e-05):
            m = jnp.mean(x, axis=-1, keepdims=True)
            v = jnp.mean((x - m) ** 2, axis=-1, keepdims=True)
            return (x - m) / jnp.sqrt(v + eps) * g + b

        def _modifier(x, w1, b1, w2, b2):
            h = jax.nn.gelu(x @ w1.T + b1, approximate=False)
            return h @ w2.T + b2

        def _reference_tuple_inner(x, ln_in_g, ln_in_b, Wk, Wv, Wq, km_w1, km_b1, km_w2, km_b2, vm_w1, vm_b1, vm_w2, vm_b2, qm_w1, qm_b1, qm_w2, qm_b2, lnk_g, lnk_b, lnv_g, lnv_b, lnq_g, lnq_b, Wo, lr_scale, Wg, bg):
            b, s, d = x.shape
            xn = _ln(x, ln_in_g, ln_in_b)
            k = xn @ Wk.T + 0.1 * _modifier(xn, km_w1, km_b1, km_w2, km_b2)
            v = xn @ Wv.T + 0.1 * _modifier(xn, vm_w1, vm_b1, vm_w2, vm_b2)
            q = xn @ Wq.T + 0.1 * _modifier(xn, qm_w1, qm_b1, qm_w2, qm_b2)
            k = _ln(k.reshape(b, s, H, HD), lnk_g, lnk_b)
            v = _ln(v.reshape(b, s, H, HD), lnv_g, lnv_b)
            q = _ln(q.reshape(b, s, H, HD), lnq_g, lnq_b)
            k_s = jnp.transpose(k, (1, 0, 2, 3))
            v_s = jnp.transpose(v, (1, 0, 2, 3))
            q_s = jnp.transpose(q, (1, 0, 2, 3))
            lr = jax.nn.sigmoid(lr_scale) * LR * 2.0
            M0 = jnp.zeros((b, H, HD, HD), x.dtype)

            def step(M, kvq):
                k_t, v_t, q_t = kvq
                out_t = jnp.einsum('bhdk,bhk->bhd', M, q_t)
                kn = k_t / (jnp.linalg.norm(k_t, axis=-1, keepdims=True) + 1e-06)
                pred = jnp.einsum('bhdk,bhk->bhd', M, kn)
                surprise = pred - v_t
                coef = pred + lr[None, :, None] * surprise
                M_new = M - jnp.einsum('bhd,bhk->bhdk', coef, kn)
                return (M_new, out_t)
            M_final, outs = jax.lax.scan(step, M0, (k_s, v_s, q_s))
            out = jnp.transpose(outs, (1, 0, 2, 3)).reshape(b, s, H * HD)
            out = out @ Wo.T
            gate = jax.nn.sigmoid(x @ Wg.T + bg)
            out = gate * out
            return (out, M_final)
        return _reference_tuple_inner(x, ln_in_g, ln_in_b, Wk, Wv, Wq, km_w1, km_b1, km_w2, km_b2, vm_w1, vm_b1, vm_w2, vm_b2, qm_w1, qm_b1, qm_w2, qm_b2, lnk_g, lnk_b, lnv_g, lnv_b, lnq_g, lnq_b, Wo, lr_scale, Wg, bg)[0]

    def _L0_ffn_ref(x, W1, b1, W2, b2, Wo, bo, gamma, beta):
        import jax, jax.numpy as jnp
        import numpy as np
        HIDDEN = 192
        INNER = 128
        EPS = 1e-05
        h = jax.nn.relu(jnp.einsum('bsd,id->bsi', x, W1) + b1)
        pred = jnp.einsum('bsi,di->bsd', h, W2) + b2
        out = jnp.einsum('bsd,ed->bse', pred, Wo) + bo
        mu = jnp.mean(out, axis=-1, keepdims=True)
        var = jnp.mean(jnp.square(out - mu), axis=-1, keepdims=True)
        out = (out - mu) * jax.lax.rsqrt(var + EPS) * gamma + beta
        return out
    h = _L0_tok_ref(x, L0_tok_Wq, L0_tok_bq, L0_tok_Wk, L0_tok_bk, L0_tok_Wv, L0_tok_bv, L0_tok_ln_g, L0_tok_ln_b, L0_tok_p1_w, L0_tok_p1_b, L0_tok_w0, L0_tok_b0, L0_tok_w1, L0_tok_b1, L0_tok_w2, L0_tok_b2, L0_tok_w3, L0_tok_b3, L0_tok_w4, L0_tok_b4, L0_tok_p2_w, L0_tok_p2_b)
    h = h + _L0_attn_ref(_layernorm(h, axis=-1), L0_attn_ln_in_g, L0_attn_ln_in_b, L0_attn_Wk, L0_attn_Wv, L0_attn_Wq, L0_attn_km_w1, L0_attn_km_b1, L0_attn_km_w2, L0_attn_km_b2, L0_attn_vm_w1, L0_attn_vm_b1, L0_attn_vm_w2, L0_attn_vm_b2, L0_attn_qm_w1, L0_attn_qm_b1, L0_attn_qm_w2, L0_attn_qm_b2, L0_attn_lnk_g, L0_attn_lnk_b, L0_attn_lnv_g, L0_attn_lnv_b, L0_attn_lnq_g, L0_attn_lnq_b, L0_attn_Wo, L0_attn_lr_scale, L0_attn_Wg, L0_attn_bg)
    h = h + _L0_ffn_ref(_layernorm(h, axis=-1), L0_ffn_W1, L0_ffn_b1, L0_ffn_W2, L0_ffn_b2, L0_ffn_Wo, L0_ffn_bo, L0_ffn_gamma, L0_ffn_beta)
    return h

_drawn_inputs = setup_inputs


def setup_inputs(seed=0):
    import zlib

    import numpy as np

    out = dict(_drawn_inputs(seed))
    spreads = {'L0_tok_ln_g': (1.0, 0.2),
     'L0_tok_ln_b': (0.0, 0.1),
     'L0_attn_ln_in_g': (1.0, 0.2),
     'L0_attn_ln_in_b': (0.0, 0.1),
     'L0_attn_km_b1': (0.0, 0.8),
     'L0_attn_km_b2': (0.0, 0.481),
     'L0_attn_vm_b1': (0.0, 0.8),
     'L0_attn_vm_b2': (0.0, 0.658),
     'L0_attn_qm_b1': (0.0, 0.8),
     'L0_attn_qm_b2': (0.0, 0.532),
     'L0_attn_lnk_g': (1.0, 0.2),
     'L0_attn_lnk_b': (0.0, 0.1),
     'L0_attn_lnv_g': (1.0, 0.2),
     'L0_attn_lnv_b': (0.0, 0.278),
     'L0_attn_lnq_g': (1.0, 0.2),
     'L0_attn_lnq_b': (0.0, 0.1),
     'L0_attn_lr_scale': (1.0, 0.6),
     'L0_attn_bg': (0.0, 0.445),
     'L0_ffn_b1': (0.0, 0.1),
     'L0_ffn_b2': (0.0, 0.1),
     'L0_ffn_gamma': (1.0, 0.2),
     'L0_ffn_beta': (0.0, 0.1)}
    factors = {'L0_tok_bq': 8.0,
     'L0_tok_bk': 64.0,
     'L0_tok_p1_b': 4.849,
     'L0_tok_b0': 8.0,
     'L0_tok_b1': 8.0,
     'L0_tok_b2': 4.393,
     'L0_attn_km_w1': 8.0,
     'L0_attn_km_w2': 8.0,
     'L0_attn_vm_w1': 8.0,
     'L0_attn_vm_w2': 8.0,
     'L0_attn_qm_w1': 8.0,
     'L0_attn_qm_w2': 8.0}
    for name, (base, spread) in spreads.items():
        noise = np.random.default_rng([zlib.crc32(name.encode()), seed]).standard_normal(out[name].shape)
        drawn = base * np.exp(spread * noise) if base else spread * noise
        out[name] = jnp.asarray(drawn.astype(out[name].dtype))
    for name, factor in factors.items():
        out[name] = (out[name] * factor).astype(out[name].dtype)
    return out
```

```python
import concourse.bass as bass
from concourse import mybir
from contextlib import ExitStack

F32 = mybir.dt.float32
F32R = mybir.dt.float32r
ALU = mybir.AluOpType
ACT = mybir.ActivationFunctionType
AX = mybir.AxisListType.X

P = 128
BATCH = 64
NPATCH = 64
INF = 768
CH = INF // P
ATT = 192
HALF = ATT // 2
HID = 768
HC = HID // P
PAIRS = NPATCH // 2
TILES = BATCH // 2
HEADS = 12
HD = 64
KD = HEADS * HD
ALL = 3 * KD
GROUPS = ALL // HD
MOD = ATT // 4
R2 = ATT - P
AUG = R2 + MOD + 1
INNER = 128
BLK = 16
NBLK = P // BLK
EPS = 1e-5
PIECES = [(0, 512, 0), (512, 256, 0), (768, 256, 1), (1024, 512, 1), (1536, 512, 2), (2048, 256, 2)]

SIGNALS = """
 chain_in0 chain_in1 chain_in2 par_in cw_in bt_mm bt_copied bt_ready eff_mm eff_ready ffn_mm ffn_cols ffn_ready lr_exp
 lr_one lr_sig lr_ready beta_ready gl_ready ones_set cw_scaled cw_sum cw_mean cw_centred cw_hi cw_ready wx_in0 wx_in1
 bias_in0 bias_in1 h_out0 h_out1 qkv_done qk_mm v_mm qk_copied v_copied tqk_mm qkT_ready scores_mm rmax_ready
 nmax_ready expP_ready pt_mm pt_copied attn_mm attn_ready bstat_ready bvar_ready bvareps_ready brstd_ready bhat_ready
 bhatg_ready att_ready attT_mm attT_copied proj_mm zmax_ready zneg_ready zexp_ready zrec_ready h_ready cstat_ready
 cvar_ready c1 c2 c3 c4 c5 crstd_ready x_ready xh_ready xT_mm xlin_copied xgate_copied mod_mm mod_ready gate_mm
 gate_ready xr_hi xr_ready proj3_mm sq_ready ssq_ready rs_var ssm_ready rs_ready kq_ready vs_ready vg_ready vb_ready kqT_mm
 kqT_ready ksq_ready norm_mm norm_copied n1 n2 n3 n4 rn_ready rscale_ready ga_mm n_ready at_ready gather_done sub_mul
 sub_step d_ready scatter_done inv_stored n_stored f_mm et_ready y_mm y_ready app_mm c_ready out_mm outT_ready wo_mm gated_ready h2_ready
 t1 y2_ready y2T_mm y2T_ready f1_mm f1_ready f2_mm fstat_ready fvar_ready fhat_ready fg_ready fb_ready f2_read
 tstat_ready tvar_ready y8_mm prec_ready hp_in0 hp_in1 hr_in0 hr_in1 t_eps f_eps t_rstd f_rstd region_ready
 att_bias_ready powers_set probs_zero res_ready out0 out1
""".split()


class Step:

    def __init__(self, it, u, off=0):
        self.n = it * 2 + (u - off)
        self.half = it + (u - off) // 2
        self.par = (u - off) % 2
        self.known = isinstance(it, int)

    def inside(self, count):
        return not self.known or 0 <= self.n < count

    def after(self, back):
        return not self.known or self.n >= back


def pipeline(engine, count, depth, step):
    lead = depth
    for s in range(2 * lead):
        step(s // 2, s % 2)
    with engine.Fori(lead, count // 2) as it:
        step(it, 0)
        step(it, 1)
    for s in range(count, count + depth):
        step(s // 2, s % 2)


def build(nc, d, out):
    with ExitStack() as ctx:
        def sb(name, shape, dt=F32):
            return ctx.enter_context(nc.sbuf_tensor(name, shape, dt))

        S = {n: ctx.enter_context(nc.semaphore(n)) for n in SIGNALS}
        PS = ctx.enter_context(nc.psum_tensor("PS", [P, 8, 512], F32))
        n_dram = nc.dram_tensor("n_scratch", (NBLK, HEADS, BLK, BLK), F32, kind="Internal").ap()
        i_dram = nc.dram_tensor("i_scratch", (NBLK, HEADS, BLK, BLK), F32, kind="Internal").ap()
        h_dram = nc.dram_tensor("h_scratch", (BATCH, NPATCH, ATT), F32, kind="Internal").ap()

        cst = sb("cst", [P, 4 * P + 2])
        ident, mask_n, mask_a, mask_e = [cst[:, i * P:(i + 1) * P] for i in range(4)]
        head_ones = cst[:, 4 * P:4 * P + 2]
        vecs = sb("vecs", [P, 12])
        lnin_g1, lnin_g2, lnin_b1, lnin_b2 = [vecs[:, i:i + 1] for i in range(4)]
        lnk_g, lnk_b, lnq_g, lnq_b = [vecs[:, i:i + 1] for i in range(4, 8)]
        ffn_b1 = vecs[:, 8:9]
        att_bias = sb("att_bias", [HALF, 4])
        mod_bias = sb("mod_bias", [P, 3])
        tok_g = sb("tok_g", [P, ATT])
        gamma = sb("gamma", [P, ATT])
        beta = sb("beta", [P, ATT])
        ffn_bias = sb("ffn_bias", [P, ATT])
        ffn_b2 = sb("ffn_b2", [HALF, 2])
        ffn_b2w = sb("ffn_b2w", [HALF, 2, P])
        lnv = sb("lnv", [P, 2, HD])
        lrs = sb("lrs", [P, HEADS])
        lr = sb("lr", [P, HEADS])
        beta_h = sb("beta_h", [P, HEADS])
        gl = sb("gl", [P, KD])
        bl = sb("bl", [P, KD])

        p1w = sb("p1w", [P, CH, ATT])
        weff1 = sb("weff1", [HALF, ATT])
        weff2 = sb("weff2", [HALF + 1, ATT])
        mod1a = sb("mod1a", [P, 3 * MOD])
        mod1b = sb("mod1b", [R2, 3 * MOD])
        gate_a = sb("gate_a", [P, ATT])
        gate_b = sb("gate_b", [R2 + 1, ATT])
        wo = sb("wo", [P, HEADS // 2, ATT])
        ffn1a = sb("ffn1a", [P, INNER])
        ffn1b = sb("ffn1b", [R2, INNER])
        ffn_w2 = sb("ffn_w2", [HALF, 2, INNER])
        ffn_wo = sb("ffn_wo", [HALF, 2, ATT])
        ffn2 = sb("ffn2", [INNER, ATT])
        cw_hi = sb("cw_hi", [P, 2, ALL], F32R)
        cw_lo = sb("cw_lo", [P, 2, ALL], F32R)

        region = sb("region", [P, 31600])
        used = {"first": 0, "second": 0}

        def part(phase, parts, *dims):
            size = 1
            for n in dims:
                size *= n
            ap = region[0:parts, used[phase]:used[phase] + size]
            used[phase] += size
            assert used[phase] <= 31600, used
            if len(dims) == 2:
                ap = ap.rearrange("p (a b) -> p a b", a=dims[0])
            if len(dims) == 3:
                ap = ap.rearrange("p (a b c) -> p a b c", a=dims[0], b=dims[1])
            if len(dims) == 4:
                ap = ap.rearrange("p (a b c e) -> p a b c e", a=dims[0], b=dims[1], c=dims[2])
            return ap

        wt = [part("first", P, 2, 3, CH, ATT) for _ in range(2)]
        xt = [part("first", P, CH, P) for _ in range(2)]
        qk_bias = [part("first", HALF, 2, 4) for _ in range(2)]
        bv = [part("first", P, ATT) for _ in range(2)]
        qk = part("first", P, 2 * ATT)
        v = [part("first", P, ATT) for _ in range(2)]
        qkT = part("first", HALF, 4, P)
        rmax = part("first", P, 1)
        nmax = part("first", P, 1)
        prob_sum = part("first", P, 1)
        prob_rec = part("first", P, 1)
        probs = part("first", P, P)
        probsT = part("first", P, P)
        attn = part("first", P, ATT)
        bstat = part("first", P, 6)
        bvar = part("first", P, 2)
        bvare = part("first", P, 1)
        brstd = part("first", P, 1)
        bhat = part("first", P, ATT)
        bhatg = part("first", P, ATT)
        att = part("first", P, ATT)
        attT1 = part("first", HALF, P)
        attT2 = part("first", HALF + 1, P)
        zmax = part("first", P, 1)
        zneg = part("first", P, 1)
        zsum = part("first", P, 1)
        zrec = part("first", P, 1)
        zexp = part("first", P, ATT)
        hb = [part("first", P, ATT) for _ in range(2)]
        bt = [part("first", P, HC, ATT + 1) for _ in range(2)]
        chain_w = [part("first", P, HC, HID) for _ in range(2)]
        chain_w4 = part("first", P, HC, ATT)
        chain_b = sb("chain_b", [P, 3, HC])
        p2a = sb("p2a", [HALF, ATT])
        p2b = sb("p2b", [HALF + 1, ATT])
        b4r = sb("b4r", [HALF + 1, ATT])
        powers = sb("powers", [P, 6, GROUPS])
        cw = chain_w[1].rearrange("p a b -> p (a b)").rearrange("p (k n) -> p k n", k=2)
        cw_sum = sb("cw_sum", [P, 2, GROUPS])
        cw_mean = sb("cw_mean", [P, 2, GROUPS])

        hp = [part("second", P, ATT) for _ in range(2)]
        hr = [part("second", P, ATT) for _ in range(2)]
        cstat = part("second", P, 6)
        cvar = part("second", P, 2)
        rstd_parts = part("second", P, 8)
        xn = part("second", P, ATT)
        xh = part("second", P, ATT)
        x_aug = part("second", P, 4, P)
        xg1 = part("second", P, P)
        xg2 = part("second", R2 + 1, P)
        gate = [part("second", P, ATT) for _ in range(2)]
        sq = part("second", P, ALL)
        ssq = part("second", P, GROUPS)
        ssm = part("second", P, GROUPS)
        rs_var = part("second", P, GROUPS)
        rs = part("second", P, GROUPS)
        kq = part("second", P, 2 * KD)
        vs = part("second", P, KD)
        vg = part("second", P, KD)
        vb = part("second", P, KD)
        kqT = part("second", P, HEADS // 2, 2, P)
        ksq = part("second", P, HEADS // 2, P)
        norm = part("second", P, 6, HEADS)
        rhs = [part("second", P, KD) for _ in range(2)]
        nmat = part("second", P, HEADS, P)
        amat = [part("second", P, HEADS, P) for _ in range(2)]
        dT = part("second", P, HEADS, P)
        blocks = part("second", NBLK * HEADS, BLK, BLK)
        inv = part("second", NBLK * HEADS, BLK, BLK)
        prod = part("second", NBLK * HEADS, BLK, BLK)
        eT = part("second", P, HEADS, P)
        y = part("second", P, KD)
        c = [part("second", P, KD) for _ in range(2)]
        outT = part("second", P, HEADS // 2, P)
        gated = part("second", P, ATT)
        h2 = part("second", P, ATT)
        tstat = part("second", P, 6)
        tvar = part("second", P, 2)
        tr = part("second", P, 4)
        y2 = part("second", P, ATT)
        y2T1 = part("second", P, P)
        y2T2 = part("second", R2, P)
        f1 = part("second", P, P)
        f2 = part("second", P, ATT)
        fstat = part("second", P, 6)
        fvar = part("second", P, 2)
        fhat = part("second", P, ATT)
        fg = part("second", P, ATT)
        fb = part("second", P, ATT)
        res = [part("second", P, ATT) for _ in range(2)]
        xr_hi = sb("xr_hi", [P, 4, P], F32R)
        xr_lo = sb("xr_lo", [P, 4, P], F32R)

        block = ctx.enter_context(nc.Block())

        def settled(engine):
            engine.nop(nofuse=True)

        @block.sync
        def _(sp):
            small = [(cst[:, :], d["consts"]), (vecs[:, 0:9], d["vecs"]), (vecs[0:R2, 9:11], d["vecs2"]),
                     (att_bias[:, :], d["att_bias"]), (mod_bias[R2:R2 + MOD, :], d["mod_bias"]),
                     (tok_g[:, :], d["tok_g"].to_broadcast([P, ATT])), (gamma[:, :], d["gamma"].to_broadcast([P, ATT])),
                     (beta[:, :], d["beta"].to_broadcast([P, ATT])), (ffn_bias[:, :], d["bo"].to_broadcast([P, ATT])),
                     (ffn_b2[:, :], d["ffn_b2"]), (lnv[:, 0, :], d["lnv_g"].to_broadcast([P, HD])),
                     (lnv[:, 1, :], d["lnv_b"].to_broadcast([P, HD])), (lrs[:, :], d["lr_scale"].to_broadcast([P, HEADS])),
                     (chain_b[:, :, :], d["chain_b"]), (p2a[:, :], d["p2"][0:HALF]), (p2b[:, :], d["p2"][HALF:ATT + 1]),
                     (b4r[HALF:HALF + 1, :], d["b4"]), (ffn_w2[:, :, :], d["ffn_w2"]), (ffn_wo[:, :, :], d["ffn_wo"]),
                     (p1w[:, :, :], d["p1_w"])]
            for dst, src in small:
                sp.dma_start(dst, src).then_inc(S["par_in"], 16)
            sp.dma_start(bt[0][:, :, :], d["w0T"]).then_inc(S["chain_in0"], 16)
            sp.dma_start(chain_w[0][:, :, :], d["w1"]).then_inc(S["chain_in0"], 16)
            sp.dma_start(chain_w[1][:, :, :], d["w2"]).then_inc(S["chain_in1"], 16)
            sp.dma_start(chain_w4[:, :, :], d["w4"]).then_inc(S["chain_in1"], 16)

            def load_biases(t):
                if t.after(2):
                    sp.wait_ge(S["attn_ready"], t.n - 1)
                    settled(sp)
                sp.dma_start(qk_bias[t.par][:, :, :], d["bqk"][t.n]).then_inc(S[f"bias_in{t.par}"], 16)
                for e in range(2):
                    sp.dma_start(bv[t.par][e * 64:e * 64 + 64, :], d["bv"][t.n, e].to_broadcast([64, ATT]))\
                      .then_inc(S[f"bias_in{t.par}"], 16)

            def load_pair(t):
                for j, (name, used_by) in enumerate((("Wq", "qk_mm"), ("Wk", "qk_mm"), ("Wv", "v_mm"))):
                    if t.after(2) and j != 1:
                        sp.wait_ge(S[used_by], t.n - 1)
                        settled(sp)
                    sp.dma_start(wt[t.par][:, :, j, :, :], d[name].rearrange("m e p c a -> m p e c a")[t.n])\
                      .then_inc(S[f"wx_in{t.par}"], 16)
                if t.after(2):
                    sp.wait_ge(S["qkv_done"], t.n - 1)
                    settled(sp)
                sp.dma_start(xt[t.par][:, :, :], d["x"][t.n]).then_inc(S[f"wx_in{t.par}"], 16)

            def store_h(t):
                sp.wait_ge(S["h_ready"], t.n + 1)
                settled(sp)
                for e in range(2):
                    sp.dma_start(h_dram.rearrange("b (m e) f -> m e b f", e=2)[t.n, e], hb[t.par][e * 64:e * 64 + 64, :])\
                      .then_inc(S[f"h_out{t.par}"], 16)

            load_pair(Step(0, 0))
            load_biases(Step(0, 0))
            sp.wait_ge(S["bt_copied"], 1)
            settled(sp)
            sp.dma_start(chain_w[0][:, :, :], d["w3"]).then_inc(S["chain_in2"], 16)
            load_pair(Step(0, 1))
            sp.wait_ge(S["bt_copied"], 2)
            settled(sp)
            for dst, src in [(cw[:, 0, :], d["kqvT"][0:P]), (cw[0:R2, 1, :], d["kqvT"][P:ATT]),
                             (cw[R2:AUG, 1, :], d["modT"]), (mod1a[:, :], d["mod1T"][0:P]), (mod1b[:, :], d["mod1T"][P:ATT]),
                             (gate_a[:, :], d["gateT"][0:P]), (gate_b[:, :], d["gateT"][P:ATT + 1]), (wo[:, :, :], d["WoT"]),
                             (ffn1a[:, :], d["ffn1T"][0:P]), (ffn1b[:, :], d["ffn1T"][P:ATT])]:
                sp.dma_start(dst, src).then_inc(S["cw_in"], 16)

            def step_b(it, u):
                t = Step(it, u)
                if t.inside(PAIRS):
                    load_pair(t)
                t = Step(it, u, 1)
                if t.inside(PAIRS):
                    load_biases(t)
                c2 = Step(it, u, 4)
                if c2.after(0):
                    store_h(c2)

            step_b(1, 0)
            step_b(1, 1)
            with sp.Fori(2, PAIRS // 2) as it:
                step_b(it, 0)
                step_b(it, 1)
            for s in range(PAIRS, PAIRS + 4):
                step_b(s // 2, s % 2)
            sp.wait_ge(S["h_out0"], PAIRS // 2 * 32)
            sp.wait_ge(S["h_out1"], PAIRS // 2 * 32)
            settled(sp)

            h_tiles = h_dram.rearrange("(t e) n f -> t (e n) f", e=2)
            out_tiles = out.rearrange("(t e) n f -> t (e n) f", e=2)

            def step_c(it, u):
                k = Step(it, u, 2)
                if k.after(0):
                    sp.wait_ge(S["d_ready"], k.n + 1)
                    settled(sp)
                    sp.dma_start(i_dram.rearrange("b h c t -> (b h) c t"), inv[:, :, :]).then_inc(S["inv_stored"], 16)
                    sp.wait_ge(S["inv_stored"], 16 * k.n + 16)
                    settled(sp)
                    if k.after(1):
                        sp.wait_ge(S["y_mm"], k.n)
                    settled(sp)
                    for b in range(NBLK):
                        sp.dma_start(dT[b * BLK:b * BLK + BLK, :, b * BLK:b * BLK + BLK],
                                     i_dram[b].rearrange("h c t -> c h t")).then_inc(S["scatter_done"], 16)
                    if k.after(2):
                        sp.wait_ge(S["h2_ready"], k.n - 1)
                    settled(sp)
                    sp.dma_start(hr[k.par][:, :], h_tiles[k.n]).then_inc(S[f"hr_in{k.par}"], 16)
                f = Step(it, u, -1)
                if not f.known or f.n < TILES:
                    if f.after(2):
                        sp.wait_ge(S["x_ready"], f.n - 1)
                    settled(sp)
                    sp.dma_start(hp[f.par][:, :], h_tiles[f.n]).then_inc(S[f"hp_in{f.par}"], 16)
                o = Step(it, u, 3)
                if o.after(0):
                    sp.wait_ge(S["res_ready"], o.n + 1)
                    settled(sp)
                    sp.dma_start(out_tiles[o.n], res[o.par][:, :]).then_inc(S[f"out{o.par}"], 16)
                j = Step(it, u, 1)
                if j.after(0) and (not j.known or j.n < TILES):
                    sp.wait_ge(S["n_ready"], (j.n + 1) * HEADS)
                    settled(sp)
                    if j.after(1):
                        sp.wait_ge(S["gather_done"], 16 * j.n)
                    settled(sp)
                    for b in range(NBLK):
                        sp.dma_start(n_dram[b].rearrange("h t j -> t h j"),
                                     nmat[b * BLK:b * BLK + BLK, :, b * BLK:b * BLK + BLK]).then_inc(S["n_stored"], 16)
                    sp.wait_ge(S["n_stored"], (16 * j.n + 16) * NBLK)
                    settled(sp)
                    if j.after(1):
                        sp.wait_ge(S["d_ready"], j.n)
                    settled(sp)
                    sp.dma_start(blocks[:, :, :], n_dram.rearrange("b h t j -> (b h) t j")).then_inc(S["gather_done"], 16)

            sp.dma_start(hp[0][:, :], h_tiles[0]).then_inc(S["hp_in0"], 16)
            for s in range(4):
                step_c(s // 2, s % 2)
            with sp.Fori(2, TILES // 2 - 1) as it:
                step_c(it, 0)
                step_c(it, 1)
            for s in range(TILES - 2, TILES + 2):
                step_c(s // 2, s % 2)
            o = Step(TILES // 2 - 1, 1)
            sp.wait_ge(S["res_ready"], o.n + 1)
            settled(sp)
            sp.dma_start(out_tiles[o.n], res[o.par][:, :]).then_inc(S["out1"], 16)
            sp.wait_ge(S["out0"], TILES // 2 * 16)
            sp.wait_ge(S["out1"], TILES // 2 * 16)
            settled(sp)

        @block.tensor
        def _(pe):
            def mm(dst, lhsT, rhs, first=True, last=True):
                return nc.tensor.matmul(dst, lhsT, rhs, start=first, stop=last)

            chain_in = ["chain_in0", "chain_in1", "chain_in2"]
            chain_count = [32, 32, 16]
            for k in range(3):
                pe.wait_ge(S[chain_in[k]], chain_count[k])
                if k:
                    pe.wait_ge(S["bt_ready"], k)
                w = chain_w[k % 2]
                for i in range(HC):
                    dst = PS[:, i // 2, (i % 2) * (ATT + 1):(i % 2 + 1) * (ATT + 1)]
                    for c_ in range(HC):
                        last = mm(dst, w[:, c_, i * P:(i + 1) * P], bt[k % 2][:, c_, :], c_ == 0, c_ == HC - 1)
                last.then_inc(S["bt_mm"], 1)
            pe.wait_ge(S["bt_ready"], 3)
            for c_ in range(HC):
                mm(PS[0:HALF, 3, 0:ATT], bt[1][:, c_, 0:HALF], chain_w4[:, c_, :], c_ == 0, c_ == HC - 1)
            for c_ in range(HC):
                last = mm(PS[0:HALF + 1, 4, 0:ATT], bt[1][:, c_, HALF:ATT + 1], chain_w4[:, c_, :], c_ == 0, c_ == HC - 1)
            last.then_inc(S["eff_mm"], 1)
            pe.wait_ge(S["par_in"], 20 * 16)
            pe.wait_ge(S["ffn_cols"], 1)
            for c_ in range(2):
                mm(PS[:, 5, 0:ATT], ffn_w2[:, c_, :], ffn_wo[:, c_, :], c_ == 0, c_ == 1)
            for c_ in range(2):
                last = mm(PS[:, 6, 0:ATT], ffn_b2w[:, c_, :], ffn_wo[:, c_, :], c_ == 0, c_ == 1)
            last.then_inc(S["ffn_mm"], 1)

            pe.wait_ge(S["eff_ready"], 3)
            pe.wait_ge(S["ones_set"], 1)
            pe.wait_ge(S["ffn_ready"], 2)

            def step_b(it, u):
                t, a, c2 = Step(it, u), Step(it, u, 1), Step(it, u, 2)
                new, mid, old = t.inside(PAIRS), a.inside(PAIRS), c2.inside(PAIRS)

                def qk_chunk(c_):
                    for e in range(2):
                        last = mm(PS[64 * e:64 * e + 64, 0, 0:2 * ATT], xt[t.par][:, c_, 64 * e:64 * e + 64],
                                  wt[t.par][:, e, 0:2, c_, :], c_ == 0, c_ == CH - 1)
                    if c_ == CH - 1:
                        last.then_inc(S["qk_mm"], 1)

                def v_chunk(c_):
                    for e in range(2):
                        last = mm(PS[64 * e:64 * e + 64, 1 + t.par, 0:ATT], xt[t.par][:, c_, 64 * e:64 * e + 64],
                                  wt[t.par][:, e, 2, c_, :], c_ == 0, c_ == CH - 1)
                    if c_ == CH - 1:
                        last.then_inc(S["v_mm"], 1)

                def p1_chunk(c_):
                    last = mm(PS[:, 1 + t.par, ATT:2 * ATT], xt[t.par][:, c_, :], p1w[:, c_, :], c_ == 0, c_ == CH - 1)
                    if c_ == CH - 1:
                        last.then_inc(S["qkv_done"], 1)

                if new:
                    pe.wait_ge(S[f"wx_in{t.par}"], (t.half + 1) * 64)
                    if t.after(1):
                        pe.wait_ge(S["qk_copied"], t.n)
                    qk_chunk(0)
                    qk_chunk(1)
                if mid:
                    pe.wait_ge(S["qk_copied"], a.n + 1)
                    if a.after(1):
                        pe.wait_ge(S["qkT_ready"], a.n)
                    for k in range(4):
                        last = nc.tensor.transpose(PS[0:HALF, 3, k * P:(k + 1) * P], qk[:, k * HALF:(k + 1) * HALF], ident)
                    last.then_inc(S["tqk_mm"], 1)
                if new:
                    for c_ in range(2, CH):
                        qk_chunk(c_)
                if mid:
                    pe.wait_ge(S["qkT_ready"], a.n + 1)
                    if a.after(1):
                        pe.wait_ge(S["expP_ready"], 2 * a.n)
                    for e in range(2):
                        for k in range(2):
                            last = mm(PS[64 * e:64 * e + 64, 4, 0:64], qkT[:, k, 64 * e:64 * e + 64],
                                      qkT[:, 2 + k, 64 * e:64 * e + 64], k == 0, k == 1)
                    last.then_inc(S["scores_mm"], 1)
                if old:
                    pe.wait_ge(S["att_ready"], c2.n + 1)
                    if c2.after(1):
                        pe.wait_ge(S["zexp_ready"], c2.n)
                    nc.tensor.transpose(PS[0:HALF, 7, 0:P], att[:, 0:HALF], ident)
                    nc.tensor.transpose(PS[0:HALF, 7, P:2 * P], att[:, HALF:ATT], ident).then_inc(S["attT_mm"], 1)
                if new:
                    if t.after(2):
                        pe.wait_ge(S["v_copied"], t.n - 1)
                        pe.wait_ge(S["att_ready"], t.n - 1)
                    for c_ in range(3):
                        v_chunk(c_)
                if old:
                    pe.wait_ge(S["attT_copied"], 2 * c2.n + 2)
                    mm(PS[:, 7, 2 * P:2 * P + ATT], attT1[:, :], weff1[:, :], True, False)
                    mm(PS[:, 7, 2 * P:2 * P + ATT], attT2[:, :], weff2[:, :], False, True).then_inc(S["proj_mm"], 1)
                if new:
                    for c_ in range(3, CH):
                        v_chunk(c_)
                    for c_ in range(3):
                        p1_chunk(c_)
                if mid:
                    pe.wait_ge(S["expP_ready"], 2 * a.n + 2)
                    if a.after(1):
                        pe.wait_ge(S["pt_copied"], a.n)
                    nc.tensor.transpose(PS[:, 5, 0:P], probs[:, :], ident).then_inc(S["pt_mm"], 1)
                if new:
                    for c_ in range(3, CH):
                        p1_chunk(c_)
                if mid:
                    pe.wait_ge(S["pt_copied"], a.n + 1)
                    pe.wait_ge(S["v_copied"], a.n + 1)
                    if a.after(1):
                        pe.wait_ge(S["attn_ready"], a.n)
                    mm(PS[:, 6, 0:ATT], probsT[:, :], v[a.par][:, :]).then_inc(S["attn_mm"], 1)

            for s in range(2):
                step_b(s // 2, s % 2)
            with pe.Fori(1, PAIRS // 2) as it:
                step_b(it, 0)
                step_b(it, 1)
            for s in range(PAIRS, PAIRS + 2):
                step_b(s // 2, s % 2)

            pe.wait_ge(S["cw_ready"], 2)
            pe.wait_ge(S["zexp_ready"], PAIRS)
            pe.wait_ge(S["attn_ready"], PAIRS)

            def turn_x(t):
                pe.wait_ge(S["xh_ready"], t.n + 1)
                for k, src in enumerate((xh, xn)):
                    nc.tensor.transpose(PS[:, 5, 2 * k * P:2 * k * P + P], src[:, 0:P], ident)
                    last = nc.tensor.transpose(PS[0:R2, 5, 2 * k * P + P:2 * k * P + 2 * P], src[:, P:ATT], ident)
                last.then_inc(S["xT_mm"], 1)

            def modifier(t):
                pe.wait_ge(S["xlin_copied"], 2 * t.n + 2)
                for j in range(3):
                    dst = PS[R2:R2 + MOD, 6, j * P:(j + 1) * P]
                    mm(dst, mod1a[:, j * MOD:(j + 1) * MOD], x_aug[:, 0, :], True, False)
                    last = mm(dst, mod1b[:, j * MOD:(j + 1) * MOD], x_aug[0:R2, 1, :], False, True)
                last.then_inc(S["mod_mm"], 1)

            def gates(t):
                pe.wait_ge(S["xgate_copied"], 2 * t.n + 2)
                if t.after(2):
                    pe.wait_ge(S["gated_ready"], t.n - 1)
                mm(PS[:, 7, 0:ATT], xg1[:, :], gate_a[:, :], True, False)
                mm(PS[:, 7, 0:ATT], xg2[:, :], gate_b[:, :], False, True).then_inc(S["gate_mm"], 1)

            def project(t):
                pe.wait_ge(S["xr_ready"], t.n + 1)
                if t.after(1):
                    pe.wait_ge(S["n_ready"], t.n * HEADS)
                    pe.wait_ge(S["at_ready"], t.n * 6)
                for col, width, j in PIECES:
                    dst = PS[:, col // 512, col % 512:col % 512 + width]
                    n = 0
                    for k, parts in ((0, P), (1, AUG)):
                        for xs, ws in ((xr_hi, cw_hi), (xr_hi, cw_lo), (xr_lo, cw_hi)):
                            slot = 0 if k == 0 else 1 + j
                            last = mm(dst, xs[0:parts, slot, :], ws[0:parts, k, col:col + width], n == 0, n == 5)
                            n += 1
                    if col != 512:
                        last.then_inc(S["proj3_mm"], 1)

            def turn_kq(t):
                pe.wait_ge(S["kq_ready"], 2 * t.n + 2)
                for k in range(12):
                    last = nc.tensor.transpose(PS[:, k // 4, (k % 4) * P:(k % 4 + 1) * P], kq[:, k * P:(k + 1) * P], ident)
                    if k % 6 == 5:
                        last.then_inc(S["kqT_mm"], 1)

            def key_norms(t):
                pe.wait_ge(S["vs_ready"], t.n + 1)
                pe.wait_ge(S["ksq_ready"], t.n + 1)
                for hp_ in range(6):
                    last = mm(PS[:, 3, 2 * hp_:2 * hp_ + 2], ksq[:, hp_, :], head_ones)
                last.then_inc(S["norm_mm"], 1)

            def grams(t, rounds):
                pe.wait_ge(S["kqT_ready"], 2 * t.n + 2)
                pe.wait_ge(S["norm_copied"], t.n + 1)
                for r in rounds:
                    if r == 2:
                        pe.wait_ge(S["n_ready"], t.n * HEADS + 4)
                        pe.wait_ge(S["at_ready"], t.n * 6 + 2)
                    for h in range(4 * r, 4 * r + 4):
                        bank = 2 * (h % 2) + r % 2
                        at = 256 * (h // 2 % 2)
                        rows = slice(64 * (h % 2), 64 * (h % 2) + 64)
                        mm(PS[:, bank, at:at + 256], kqT[rows, h // 2, 0, :], kqT[rows, h // 2, :, :])\
                          .then_inc(S["ga_mm"], 1)

            def begin_solve(t):
                pe.wait_ge(S["scatter_done"], (t.n + 1) * NBLK * 16)
                pe.wait_ge(S["n_ready"], (t.n + 1) * HEADS)
                if t.after(1):
                    pe.wait_ge(S["f2_read"], t.n)
                if not t.known or t.n + 2 < TILES:
                    pe.wait_ge(S["xgate_copied"], 2 * t.n + 6)
                    pe.wait_ge(S["mod_ready"], 3 * t.n + 9)
                for h in range(HEADS):
                    last = mm(PS[:, 5 + h // 4, (h % 4) * P:(h % 4 + 1) * P], nmat[:, h, :], dT[:, h, :])
                    if h % 4 == 3:
                        last.then_inc(S["f_mm"], 1)
                pe.wait_ge(S["rscale_ready"], t.n + 1)
                pe.wait_ge(S["et_ready"], 3 * t.n + 1)
                for h in range(HEADS):
                    if h == 8:
                        pe.wait_ge(S["et_ready"], 3 * t.n + 2)
                    last = mm(PS[:, 5 + h // 8, (h % 8) * HD:(h % 8 + 1) * HD], dT[:, h, :], rhs[t.par][:, h * HD:(h + 1) * HD])
                    if h == 7:
                        last.then_inc(S["y8_mm"], 1)
                last.then_inc(S["y_mm"], 1)
                pe.wait_ge(S["et_ready"], 3 * t.n + 3)

            def apply(t, rounds):
                for k in rounds:
                    src = (y, c[0], c[1])[k]
                    bank, at = ((7, 256), (5, 0), (7, 256))[k]
                    for h in range(HEADS):
                        if h == 0 or h == 8:
                            pe.wait_ge(S["y_ready" if k == 0 else "c_ready"],
                                       2 * t.n + 1 + h // 8 if k == 0 else 6 * t.n + 2 * (k - 1) + 1 + h // 8)
                        dst = PS[:, bank, h * HD:(h + 1) * HD] if h < 8 else PS[:, 6, at + (h - 8) * HD:at + (h - 7) * HD]
                        last = mm(dst, eT[:, h, :], src[:, h * HD:(h + 1) * HD])
                        if h % 8 == 7 or h == 11:
                            last.then_inc(S["app_mm"], 1)

            def solved(t):
                pe.wait_ge(S["c_ready"], 6 * t.n + 6)
                for h in range(HEADS):
                    rows = slice(64 * (h % 2), 64 * (h % 2) + 64)
                    hp_ = h // 2
                    last = mm(PS[rows, 5 + hp_ // 4, (hp_ % 4) * P:(hp_ % 4 + 1) * P], c[0][:, h * HD:(h + 1) * HD], amat[t.par][:, h, :])
                last.then_inc(S["out_mm"], 1)
                pe.wait_ge(S["outT_ready"], t.n + 1)
                for hp_ in range(6):
                    last = mm(PS[:, 7, 0:ATT], outT[:, hp_, :], wo[:, hp_, :], hp_ == 0, hp_ == 5)
                last.then_inc(S["wo_mm"], 1)

            def finish(t):
                pe.wait_ge(S["y2_ready"], t.n + 1)
                if not t.known or t.n + 2 < TILES:
                    pe.wait_ge(S["gate_ready"], t.n + 3)
                    pe.wait_ge(S["mod_ready"], 3 * t.n + 9)
                nc.tensor.transpose(PS[:, 5, 0:P], y2[:, 0:P], ident)
                nc.tensor.transpose(PS[0:R2, 5, P:2 * P], y2[:, P:ATT], ident).then_inc(S["y2T_mm"], 1)
                pe.wait_ge(S["y2T_ready"], 2 * t.n + 2)
                mm(PS[:, 6, 0:P], ffn1a[:, :], y2T1[:, :], True, False)
                mm(PS[:, 6, 0:P], ffn1b[:, :], y2T2[:, :], False, True).then_inc(S["f1_mm"], 1)
                pe.wait_ge(S["f1_ready"], t.n + 1)
                mm(PS[:, 7, 0:ATT], f1[:, :], ffn2[:, :]).then_inc(S["f2_mm"], 1)

            def step_c(it, u):
                t, j, k = Step(it, u), Step(it, u, 1), Step(it, u, 2)
                if j.inside(TILES):
                    turn_kq(j)
                    key_norms(j)
                if t.inside(TILES):
                    turn_x(t)
                if j.inside(TILES):
                    grams(j, (0,))
                if t.inside(TILES):
                    modifier(t)
                if j.inside(TILES):
                    grams(j, (1,))
                if k.inside(TILES):
                    begin_solve(k)
                    apply(k, (0,))
                if j.inside(TILES):
                    grams(j, (2,))
                if k.inside(TILES):
                    apply(k, (1,))
                if t.inside(TILES):
                    project(t)
                if k.inside(TILES):
                    apply(k, (2,))
                    solved(k)
                if t.inside(TILES):
                    gates(t)
                if k.inside(TILES):
                    finish(k)

            pipeline(pe, TILES, 2, step_c)

        @block.scalar
        def _(act):
            act.wait_ge(S["par_in"], 20 * 16)
            act.activation(lr[:, :], lrs[:, :], ACT.Exp, scale=-1.0).then_inc(S["lr_exp"], 1)
            scale = float(ATT) ** -0.5

            def step_b(it, u):
                t, a, c2 = Step(it, u), Step(it, u, 1), Step(it, u, 2)
                if t.inside(PAIRS):
                    act.wait_ge(S["qk_mm"], t.n + 1)
                    if t.after(1):
                        act.wait_ge(S["tqk_mm"], t.n)
                    act.activation(qk[:, :], PS[:, 0, 0:2 * ATT], ACT.Copy).then_inc(S["qk_copied"], 1)
                if c2.inside(PAIRS):
                    act.wait_ge(S["attT_mm"], c2.n + 1)
                    act.wait_ge(S["att_bias_ready"], 1)
                    if c2.after(1):
                        act.wait_ge(S["proj_mm"], c2.n)
                    act.activation(attT1[:, :], PS[0:HALF, 7, 0:P], ACT.Identity, bias=att_bias[:, 0:1])\
                       .then_inc(S["attT_copied"], 1)
                    act.activation(attT2[0:HALF, :], PS[0:HALF, 7, P:2 * P], ACT.Identity, bias=att_bias[:, 1:2])\
                       .then_inc(S["attT_copied"], 1)
                if a.inside(PAIRS):
                    act.wait_ge(S["nmax_ready"], a.n + 1)
                    if a.after(1):
                        act.wait_ge(S["pt_mm"], a.n)
                        act.wait_ge(S["prec_ready"], a.n)
                    else:
                        act.wait_ge(S["probs_zero"], 1)
                    for e in range(2):
                        rows = slice(64 * e, 64 * e + 64)
                        act.activation(probs[rows, rows], PS[rows, 4, 0:64], ACT.Exp, bias=nmax[rows, :], scale=scale,
                                       accum_out=prob_sum[rows, :]).then_inc(S["expP_ready"], 1)
                if c2.inside(PAIRS):
                    act.wait_ge(S["zneg_ready"], c2.n + 1)
                    if c2.after(1):
                        act.wait_ge(S["h_ready"], c2.n)
                    act.activation(zexp[:, :], PS[:, 7, 2 * P:2 * P + ATT], ACT.Exp, bias=zneg[:, :], accum_out=zsum[:, :])\
                       .then_inc(S["zexp_ready"], 1)
                if a.inside(PAIRS):
                    act.wait_ge(S["pt_mm"], a.n + 1)
                    if a.after(1):
                        act.wait_ge(S["attn_mm"], a.n)
                    act.activation(probsT[:, :], PS[:, 5, 0:P], ACT.Copy).then_inc(S["pt_copied"], 1)
                if t.inside(PAIRS):
                    act.wait_ge(S["qkv_done"], t.n + 1)
                    if t.after(2):
                        act.wait_ge(S["attn_mm"], t.n - 1)
                    act.activation(v[t.par][:, :], PS[:, 1 + t.par, 0:ATT], ACT.Copy).then_inc(S["v_copied"], 1)

            pipeline(act, PAIRS, 2, step_b)

            act.wait_ge(S["region_ready"], 5)

            def step_c(it, u):
                t, j, k = Step(it, u), Step(it, u, 1), Step(it, u, 2)
                if j.inside(TILES):
                    front = PS[:, 0:3, :].rearrange("p a b -> p (a b)")
                    act.wait_ge(S["kqT_mm"], 2 * j.n + 1)
                    act.wait_ge(S["kqT_mm"], 2 * j.n + 2)
                    if j.after(1):
                        act.wait_ge(S["ga_mm"], HEADS * j.n)
                        act.wait_ge(S["norm_mm"], j.n)
                    act.activation(kqT[:, :, 0, :], front[:, 0:KD].rearrange("p (a b) -> p a b", a=6), ACT.Identity,
                                   scale=lnk_g, bias=lnk_b).then_inc(S["kqT_ready"], 1)
                    act.wait_ge(S["kqT_ready"], 2 * j.n + 1)
                    act.activation(ksq[:, :, :], kqT[:, :, 0, :], ACT.Square).then_inc(S["ksq_ready"], 1)
                    act.activation(kqT[:, :, 1, :], front[:, KD:2 * KD].rearrange("p (a b) -> p a b", a=6), ACT.Identity,
                                   scale=lnq_g, bias=lnq_b).then_inc(S["kqT_ready"], 1)
                if t.inside(TILES):
                    act.wait_ge(S["xT_mm"], t.n + 1)
                    if t.after(1):
                        act.wait_ge(S["xr_ready"], t.n)
                        act.wait_ge(S["gate_mm"], t.n)
                    act.activation(x_aug[:, 0, :], PS[:, 5, 0:P], ACT.Identity, scale=lnin_g1, bias=lnin_b1)\
                       .then_inc(S["xlin_copied"], 1)
                    act.activation(x_aug[0:R2, 1:4, :], PS[0:R2, 5, P:2 * P].unsqueeze(1).to_broadcast([R2, 3, P]), ACT.Identity,
                                   scale=vecs[0:R2, 9:10], bias=vecs[0:R2, 10:11]).then_inc(S["xlin_copied"], 1)
                    act.activation(xg1[:, :], PS[:, 5, 2 * P:3 * P], ACT.Copy).then_inc(S["xgate_copied"], 1)
                    act.activation(xg2[0:R2, :], PS[0:R2, 5, 3 * P:4 * P], ACT.Copy).then_inc(S["xgate_copied"], 1)
                    act.wait_ge(S["mod_mm"], t.n + 1)
                    rows = slice(R2, R2 + MOD)
                    for m in range(3):
                        act.activation(x_aug[rows, 1 + m, :], PS[rows, 6, m * P:(m + 1) * P], ACT.Gelu,
                                       bias=mod_bias[rows, m:m + 1]).then_inc(S["mod_ready"], 1)
                if k.inside(TILES):
                    act.wait_ge(S["y8_mm"], k.n + 1)
                    if k.after(1):
                        act.wait_ge(S["c_ready"], 6 * k.n)
                    act.activation(y[:, 0:8 * HD], PS[:, 5, 0:8 * HD], ACT.Copy).then_inc(S["y_ready"], 1)
                    act.wait_ge(S["y_mm"], k.n + 1)
                    act.activation(y[:, 8 * HD:KD], PS[:, 6, 0:4 * HD], ACT.Copy).then_inc(S["y_ready"], 1)
                if t.inside(TILES):
                    if t.after(1):
                        act.wait_ge(S["ssq_ready"], 2 * t.n)
                    for b in range(5):
                        act.wait_ge(S["proj3_mm"], 5 * t.n + b + 1)
                        width = min(512, ALL - 512 * b)
                        act.activation(sq[:, 512 * b:512 * b + width], PS[:, b, 0:width], ACT.Square).then_inc(S["sq_ready"], 1)
                if k.inside(TILES):
                    act.wait_ge(S["out_mm"], k.n + 1)
                    if k.after(1):
                        act.wait_ge(S["wo_mm"], k.n)
                    act.activation(outT[:, :, :], PS[:, 5:7, :].rearrange("p a b -> p (a b)")[:, 0:KD]
                                   .rearrange("p (a b) -> p a b", a=6), ACT.Copy).then_inc(S["outT_ready"], 1)
                if t.inside(TILES):
                    act.wait_ge(S["gate_mm"], t.n + 1)
                    if t.after(2):
                        act.wait_ge(S["gated_ready"], t.n - 1)
                    act.activation(gate[t.par][:, :], PS[:, 7, 0:ATT], ACT.Tanh, scale=0.5).then_inc(S["gate_ready"], 1)
                if k.inside(TILES):
                    act.wait_ge(S["y2T_mm"], k.n + 1)
                    if k.after(1):
                        act.wait_ge(S["f1_mm"], k.n)
                    act.activation(y2T1[:, :], PS[:, 5, 0:P], ACT.Copy).then_inc(S["y2T_ready"], 1)
                    act.activation(y2T2[:, :], PS[0:R2, 5, P:2 * P], ACT.Copy).then_inc(S["y2T_ready"], 1)
                    act.wait_ge(S["f1_mm"], k.n + 1)
                    if k.after(1):
                        act.wait_ge(S["f2_mm"], k.n)
                    act.activation(f1[:, :], PS[:, 6, 0:P], ACT.Relu, bias=ffn_b1).then_inc(S["f1_ready"], 1)

            pipeline(act, TILES, 2, step_c)

        @block.gpsimd
        def _(pool):
            for i, value in enumerate((-0.5, 0.5, -1.0, EPS, 1.0 / HD, 1e-6)):
                pool.memset(powers[:, i, :], value).then_inc(S["powers_set"], 1)
            pool.memset(probs[:, :], 0.0).then_inc(S["probs_zero"], 1)
            pool.wait_ge(S["probs_zero"], 1)
            pool.memset(attT2[HALF:HALF + 1, :], 1.0).then_inc(S["ones_set"], 1)
            pool.wait_ge(S["powers_set"], 6)
            pool.wait_ge(S["ones_set"], 1)
            root, square_root, inverse, eps, per_head, tiny = [powers[:, i, :] for i in range(6)]

            def step_b(it, u):
                c2 = Step(it, u, 2)
                if c2.inside(PAIRS):
                    pool.wait_ge(S["bvar_ready"], c2.n + 1)
                    pool.tensor_tensor(bvare[:, :], bvar[:, 1:2], eps[:, 0:1], ALU.add).then_inc(S["bvareps_ready"], 1)
                    pool.wait_ge(S["bvareps_ready"], c2.n + 1)
                    pool.tensor_tensor(brstd[:, :], bvare[:, :], root[:, 0:1], ALU.pow).then_inc(S["brstd_ready"], 1)

            pipeline(pool, PAIRS, 2, step_b)

            pool.wait_ge(S["h_out0"], PAIRS // 2 * 32)
            pool.wait_ge(S["h_out1"], PAIRS // 2 * 32)
            for i, (dst, value) in enumerate(((x_aug, 1.0), (xg2, 1.0), (dT, 0.0), (inv, 0.0))):
                pool.memset(dst, value).then_inc(S["region_ready"], 1)
                pool.wait_ge(S["region_ready"], i + 1)
            pool.memset(inv.rearrange("p a b -> p (a b)")[:, 0:BLK * BLK:BLK + 1], 1.0).then_inc(S["region_ready"], 1)

            def step_c(it, u):
                t, j, k = Step(it, u), Step(it, u, 1), Step(it, u, 2)
                if t.inside(TILES):
                    r = rstd_parts
                    pool.wait_ge(S["cvar_ready"], t.n + 1)
                    pool.tensor_tensor(r[:, 0:1], cvar[:, 1:2], eps[:, 0:1], ALU.add).then_inc(S["c1"], 1)
                    pool.wait_ge(S["c1"], t.n + 1)
                    pool.tensor_tensor(r[:, 1:2], r[:, 0:1], root[:, 0:1], ALU.pow).then_inc(S["c2"], 1)
                    pool.wait_ge(S["c2"], t.n + 1)
                    pool.tensor_tensor(r[:, 2:3], r[:, 1:2], r[:, 1:2], ALU.mult).then_inc(S["c3"], 1)
                    pool.wait_ge(S["c3"], t.n + 1)
                    pool.tensor_tensor(r[:, 3:4], r[:, 2:3], cvar[:, 1:2], ALU.mult).then_inc(S["c4"], 1)
                    pool.wait_ge(S["c4"], t.n + 1)
                    pool.tensor_tensor(r[:, 4:5], r[:, 3:4], eps[:, 0:1], ALU.add).then_inc(S["c5"], 1)
                    pool.wait_ge(S["c5"], t.n + 1)
                    pool.tensor_tensor(r[:, 5:6], r[:, 4:5], root[:, 0:1], ALU.pow).then_inc(S["crstd_ready"], 1)
                if j.inside(TILES):
                    pool.wait_ge(S["norm_copied"], j.n + 1)
                    if j.after(1):
                        pool.wait_ge(S["n2"], j.n)
                    pool.tensor_tensor(norm[:, 1, :], norm[:, 0, :], square_root[:, 0:HEADS], ALU.pow).then_inc(S["n1"], 1)
                if t.inside(TILES):
                    if t.after(1):
                        pool.wait_ge(S["vs_ready"], t.n)
                    for i, cols in enumerate((slice(0, 2 * HEADS), slice(2 * HEADS, GROUPS))):
                        pool.wait_ge(S["ssq_ready"], 2 * t.n + i + 1)
                        pool.tensor_tensor(ssm[:, cols], ssq[:, cols], per_head[:, cols], ALU.mult).then_inc(S["ssm_ready"], 1)
                        pool.wait_ge(S["ssm_ready"], 2 * t.n + i + 1)
                        pool.tensor_tensor(rs_var[:, cols], ssm[:, cols], eps[:, cols], ALU.add).then_inc(S["rs_var"], 1)
                        pool.wait_ge(S["rs_var"], 2 * t.n + i + 1)
                        pool.tensor_tensor(rs[:, cols], rs_var[:, cols], root[:, cols], ALU.pow).then_inc(S["rs_ready"], 1)
                if k.inside(TILES):
                    pool.wait_ge(S["tvar_ready"], k.n + 1)
                    pool.tensor_tensor(tr[:, 0:1], tvar[:, 1:2], eps[:, 0:1], ALU.add).then_inc(S["t_eps"], 1)
                    pool.wait_ge(S["t_eps"], k.n + 1)
                    pool.tensor_tensor(tr[:, 1:2], tr[:, 0:1], root[:, 0:1], ALU.pow).then_inc(S["t_rstd"], 1)
                if k.inside(TILES):
                    pool.wait_ge(S["fvar_ready"], k.n + 1)
                    pool.tensor_tensor(tr[:, 2:3], fvar[:, 1:2], eps[:, 0:1], ALU.add).then_inc(S["f_eps"], 1)
                    pool.wait_ge(S["f_eps"], k.n + 1)
                    pool.tensor_tensor(tr[:, 3:4], tr[:, 2:3], root[:, 0:1], ALU.pow).then_inc(S["f_rstd"], 1)

            pipeline(pool, TILES, 2, step_c)

        @block.vector
        def _(dve):
            dve.wait_ge(S["par_in"], 20 * 16)
            dve.wait_ge(S["lr_exp"], 1)
            dve.tensor_scalar(beta_h[:, :], lr[:, :], 1.0, None, ALU.add).then_inc(S["lr_one"], 1)
            dve.wait_ge(S["lr_one"], 1)
            dve.reciprocal(lrs[:, :], beta_h[:, :]).then_inc(S["lr_sig"], 1)
            dve.wait_ge(S["lr_sig"], 1)
            dve.tensor_scalar(lr[:, :], lrs[:, :], 0.2, None, ALU.mult).then_inc(S["lr_ready"], 1)
            dve.wait_ge(S["lr_ready"], 1)
            dve.tensor_scalar(beta_h[:, :], lr[:, :], 1.0, None, ALU.add).then_inc(S["beta_ready"], 1)
            for i, dst in enumerate((gl, bl)):
                dve.tensor_tensor(dst[:, :].rearrange("p (h d) -> p h d", d=HD),
                                  lnv[:, i, :].unsqueeze(1).to_broadcast([P, HEADS, HD]),
                                  lr[:, :].unsqueeze(2).to_broadcast([P, HEADS, HD]), ALU.mult).then_inc(S["gl_ready"], 1)
            dve.tensor_tensor(att_bias[:, 0:2], att_bias[:, 0:2], att_bias[:, 2:4], ALU.add).then_inc(S["att_bias_ready"], 1)
            dve.tensor_copy(ffn_b2w[:, :, :], ffn_b2[:, :].unsqueeze(2).to_broadcast([HALF, 2, P])).then_inc(S["ffn_cols"], 1)

            for k in range(3):
                dve.wait_ge(S["bt_mm"], k + 1)
                dst = bt[(k + 1) % 2].rearrange("p (a b) n -> p a b n", b=2)
                src = PS[:, 0:3, 0:2 * (ATT + 1)].rearrange("p a (b n) -> p a b n", b=2)
                dve.tensor_copy(dst, src).then_inc(S["bt_copied"], 1)
                dve.wait_ge(S["bt_copied"], k + 1)
                dve.tensor_tensor(bt[(k + 1) % 2][:, :, ATT], bt[(k + 1) % 2][:, :, ATT], chain_b[:, k, :], ALU.add)\
                   .then_inc(S["bt_ready"], 1)
            dve.wait_ge(S["eff_mm"], 1)
            dve.tensor_tensor(weff1[:, :], PS[0:HALF, 3, 0:ATT], p2a[:, :], ALU.add).then_inc(S["eff_ready"], 1)
            dve.tensor_tensor(weff2[:, :], PS[0:HALF + 1, 4, 0:ATT], p2b[:, :], ALU.add).then_inc(S["eff_ready"], 1)
            dve.wait_ge(S["eff_ready"], 2)
            dve.tensor_tensor(weff2[HALF:HALF + 1, :], weff2[HALF:HALF + 1, :], b4r[HALF:HALF + 1, :], ALU.add)\
               .then_inc(S["eff_ready"], 1)
            dve.wait_ge(S["ffn_mm"], 1)
            dve.tensor_copy(ffn2[:, :], PS[:, 5, 0:ATT]).then_inc(S["ffn_ready"], 1)
            dve.tensor_tensor(ffn_bias[:, :], PS[:, 6, 0:ATT], ffn_bias[:, :], ALU.add).then_inc(S["ffn_ready"], 1)

            dve.wait_ge(S["cw_in"], 160)
            dve.tensor_scalar(cw[R2:AUG, 1, :], cw[R2:AUG, 1, :], 0.1, None, ALU.mult).then_inc(S["cw_scaled"], 1)
            dve.wait_ge(S["cw_scaled"], 1)
            for k, parts in enumerate((P, AUG)):
                group = cw[0:parts, k, :].rearrange("p (g d) -> p g d", d=HD)
                dve.tensor_reduce(cw_sum[0:parts, k, :], group, AX, ALU.add).then_inc(S["cw_sum"], 1)
                dve.wait_ge(S["cw_sum"], k + 1)
                dve.tensor_scalar(cw_mean[0:parts, k, :], cw_sum[0:parts, k, :], 1.0 / HD, None, ALU.mult).then_inc(S["cw_mean"], 1)
                dve.wait_ge(S["cw_mean"], k + 1)
                dve.tensor_tensor(group, group, cw_mean[0:parts, k, :].unsqueeze(2).to_broadcast([parts, GROUPS, HD]),
                                  ALU.subtract).then_inc(S["cw_centred"], 1)
                dve.wait_ge(S["cw_centred"], k + 1)
                dve.tensor_copy(cw_hi[0:parts, k, :], cw[0:parts, k, :]).then_inc(S["cw_hi"], 1)
                dve.wait_ge(S["cw_hi"], k + 1)
                dve.tensor_tensor(cw_lo[0:parts, k, :], cw[0:parts, k, :], cw_hi[0:parts, k, :].bitcast(F32), ALU.subtract)\
                   .then_inc(S["cw_ready"], 1)

            def step_b(it, u):
                a, c2 = Step(it, u, 1), Step(it, u, 2)
                mid, old = a.inside(PAIRS), c2.inside(PAIRS)
                if old:
                    dve.wait_ge(S["attn_mm"], c2.n + 1)
                    dve.wait_ge(S[f"bias_in{c2.par}"], (c2.half + 1) * 48)
                    dve.wait_ge(S["prec_ready"], c2.n + 1)
                    dve.scalar_tensor_tensor(out=attn[:, :], in0=PS[:, 6, 0:ATT], scalar=prob_rec[:, :], in1=bv[c2.par][:, :],
                                             op0=ALU.mult, op1=ALU.add).then_inc(S["attn_ready"], 1)
                    dve.wait_ge(S["attn_ready"], c2.n + 1)
                    dve.bn_stats(bstat[:, :], attn[:, :]).then_inc(S["bstat_ready"], 1)
                    dve.wait_ge(S["bstat_ready"], c2.n + 1)
                    settled(dve)
                    dve.bn_aggr(bvar[:, :], bstat[:, :]).then_inc(S["bvar_ready"], 1)
                if mid:
                    dve.wait_ge(S["tqk_mm"], a.n + 1)
                    dve.wait_ge(S[f"bias_in{a.par}"], (a.half + 1) * 48)
                    if a.after(1):
                        dve.wait_ge(S["scores_mm"], a.n)
                    dve.tensor_tensor(qkT.rearrange("p k (e b) -> p k e b", e=2),
                                      PS[0:HALF, 3, :].rearrange("p (k e b) -> p k e b", k=4, e=2),
                                      qk_bias[a.par].rearrange("p e k -> p k e").unsqueeze(3).to_broadcast([HALF, 4, 2, 64]),
                                      ALU.add).then_inc(S["qkT_ready"], 1)
                if old:
                    dve.wait_ge(S["brstd_ready"], c2.n + 1)
                    dve.wait_ge(S["bvar_ready"], c2.n + 1)
                    dve.tensor_scalar(bhat[:, :], attn[:, :], bvar[:, 0:1], brstd[:, 0:1], ALU.subtract, ALU.mult)\
                       .then_inc(S["bhat_ready"], 1)
                    dve.wait_ge(S["bhat_ready"], c2.n + 1)
                    dve.tensor_tensor(bhatg[:, :], bhat[:, :], tok_g[:, :], ALU.mult).then_inc(S["bhatg_ready"], 1)
                    dve.wait_ge(S["bhatg_ready"], c2.n + 1)
                    if c2.after(1):
                        dve.wait_ge(S["attT_mm"], c2.n)
                    dve.tensor_tensor(att[:, :], PS[:, 1 + c2.par, ATT:2 * ATT], bhatg[:, :], ALU.add).then_inc(S["att_ready"], 1)
                if mid:
                    dve.wait_ge(S["scores_mm"], a.n + 1)
                    dve.tensor_reduce(rmax[:, :], PS[:, 4, 0:64], AX, ALU.max).then_inc(S["rmax_ready"], 1)
                    dve.wait_ge(S["rmax_ready"], a.n + 1)
                    if a.after(1):
                        dve.wait_ge(S["expP_ready"], 2 * a.n)
                    dve.tensor_scalar(nmax[:, :], rmax[:, :], -float(ATT) ** -0.5, None, ALU.mult).then_inc(S["nmax_ready"], 1)
                if old:
                    dve.wait_ge(S["proj_mm"], c2.n + 1)
                    dve.tensor_reduce(zmax[:, :], PS[:, 7, 2 * P:2 * P + ATT], AX, ALU.max).then_inc(S["zmax_ready"], 1)
                    dve.wait_ge(S["zmax_ready"], c2.n + 1)
                    if c2.after(1):
                        dve.wait_ge(S["zexp_ready"], c2.n)
                    dve.tensor_scalar(zneg[:, :], zmax[:, :], -1.0, None, ALU.mult).then_inc(S["zneg_ready"], 1)
                if mid:
                    dve.wait_ge(S["expP_ready"], 2 * a.n + 2)
                    dve.reciprocal(prob_rec[:, :], prob_sum[:, :]).then_inc(S["prec_ready"], 1)
                if old:
                    dve.wait_ge(S["zexp_ready"], c2.n + 1)
                    dve.reciprocal(zrec[:, :], zsum[:, :]).then_inc(S["zrec_ready"], 1)
                    dve.wait_ge(S["zrec_ready"], c2.n + 1)
                    if c2.after(2):
                        dve.wait_ge(S[f"h_out{c2.par}"], c2.half * 32)
                    dve.tensor_scalar(hb[c2.par][:, :], zexp[:, :], zrec[:, 0:1], None, ALU.mult).then_inc(S["h_ready"], 1)

            pipeline(dve, PAIRS, 2, step_b)

            dve.wait_ge(S["region_ready"], 5)

            def invert(k, rows):
                if rows[0] == 1:
                    dve.wait_ge(S["gather_done"], (k.n + 1) * 16)
                    if k.after(1):
                        dve.wait_ge(S["inv_stored"], k.n * 16)
                for r in rows:
                    if r > 1:
                        dve.wait_ge(S["sub_step"], k.n * (BLK - 2) + r - 1)
                    dve.tensor_tensor(prod[:, 0:r, 0:r], inv[:, 0:r, 0:r],
                                      blocks[:, r, 0:r].unsqueeze(1).to_broadcast([NBLK * HEADS, r, r]), ALU.mult)\
                       .then_inc(S["sub_mul"], 1)
                    dve.wait_ge(S["sub_mul"], k.n * (BLK - 1) + r)
                    last = dve.tensor_reduce(inv[:, 0:r, r], prod[:, 0:r, 0:r], AX, ALU.add)
                    last.then_inc(S["sub_step" if r < BLK - 1 else "d_ready"], 1)

            def moments(j, i):
                dve.wait_ge(S["sq_ready"], 5 * j.n + (3, 5)[i])
                if j.after(1):
                    dve.wait_ge(S["ssm_ready"], 2 * j.n)
                groups = (slice(0, 2 * HEADS), slice(2 * HEADS, GROUPS))[i]
                dve.tensor_reduce(ssq[:, groups], sq.rearrange("p (g d) -> p g d", d=HD)[:, groups, :], AX, ALU.add)\
                   .then_inc(S["ssq_ready"], 1)

            def scale_kq(j):
                dve.wait_ge(S["rs_ready"], 2 * j.n + 1)
                if j.after(1):
                    dve.wait_ge(S["kqT_mm"], 2 * j.n)
                front = PS[:, 0:3, :].rearrange("p a b -> p (a b)")
                for i in range(2):
                    dve.tensor_tensor(kq[:, i * KD:(i + 1) * KD].rearrange("p (g d) -> p g d", d=HD),
                                      front[:, i * KD:(i + 1) * KD].rearrange("p (g d) -> p g d", d=HD),
                                      rs[:, i * HEADS:(i + 1) * HEADS].unsqueeze(2).to_broadcast([P, HEADS, HD]), ALU.mult)\
                       .then_inc(S["kq_ready"], 1)

            def scale_v(j):
                dve.wait_ge(S["rs_ready"], 2 * j.n + 2)
                front = PS[:, 3:5, :].rearrange("p a b -> p (a b)")
                dve.tensor_tensor(vs.rearrange("p (g d) -> p g d", d=HD), front[:, 0:KD].rearrange("p (g d) -> p g d", d=HD),
                                  rs[:, 2 * HEADS:].unsqueeze(2).to_broadcast([P, HEADS, HD]), ALU.mult).then_inc(S["vs_ready"], 1)

            def shift_v(j):
                dve.wait_ge(S["vs_ready"], j.n + 1)
                dve.tensor_tensor(vg[:, :], vs[:, :], gl[:, :], ALU.mult).then_inc(S["vg_ready"], 1)
                dve.wait_ge(S["vg_ready"], j.n + 1)
                dve.tensor_tensor(vb[:, :], vg[:, :], bl[:, :], ALU.add).then_inc(S["vb_ready"], 1)

            def take_e(k):
                for i in range(3):
                    dve.wait_ge(S["f_mm"], 3 * k.n + i + 1)
                    if i == 0 and k.after(1):
                        dve.wait_ge(S["app_mm"], 6 * k.n)
                    dve.tensor_tensor(eT[:, 4 * i:4 * i + 4, :], PS[:, 5 + i, :].rearrange("p (h t) -> p h t", h=4),
                                      mask_e.unsqueeze(1).to_broadcast([P, 4, P]), ALU.mult).then_inc(S["et_ready"], 1)

            def take_c(k, n):
                bank, at = ((7, 256), (5, 0), (7, 256))[n]
                dst = c[n % 2]
                for i in range(2):
                    dve.wait_ge(S["app_mm"], 6 * k.n + 2 * n + i + 1)
                    dve.wait_ge(S["y_ready"], 2 * k.n + i + 1)
                    if n < 2 and k.after(1):
                        dve.wait_ge(S["out_mm"], k.n)
                    cols = slice(0, 8 * HD) if i == 0 else slice(8 * HD, KD)
                    src = PS[:, bank, :] if i == 0 else PS[:, 6, at:at + 4 * HD]
                    dve.tensor_tensor(dst[:, cols], src, y[:, cols], ALU.add).then_inc(S["c_ready"], 1)

            def gate_and_add(k):
                dve.wait_ge(S["wo_mm"], k.n + 1)
                dve.wait_ge(S["gate_ready"], k.n + 1)
                dve.scalar_tensor_tensor(out=gated[:, :], in0=gate[k.par][:, :], scalar=1.0, in1=PS[:, 7, 0:ATT],
                                         op0=ALU.add, op1=ALU.mult).then_inc(S["gated_ready"], 1)
                dve.wait_ge(S["gated_ready"], k.n + 1)
                dve.wait_ge(S[f"hr_in{k.par}"], (k.half + 1) * 16)
                dve.scalar_tensor_tensor(out=h2[:, :], in0=gated[:, :], scalar=0.5, in1=hr[k.par][:, :],
                                         op0=ALU.mult, op1=ALU.add).then_inc(S["h2_ready"], 1)
                dve.wait_ge(S["h2_ready"], k.n + 1)
                dve.bn_stats(tstat[:, :], h2[:, :]).then_inc(S["tstat_ready"], 1)
                dve.wait_ge(S["tstat_ready"], k.n + 1)
                settled(dve)
                dve.bn_aggr(tvar[:, :], tstat[:, :]).then_inc(S["tvar_ready"], 1)

            def norm_h2(k):
                dve.wait_ge(S["t_rstd"], k.n + 1)
                dve.wait_ge(S["tvar_ready"], k.n + 1)
                dve.tensor_scalar(y2[:, :], h2[:, :], tvar[:, 0:1], tr[:, 1:2], ALU.subtract, ALU.mult).then_inc(S["y2_ready"], 1)

            def take_a(j, r):
                if j.after(2):
                    dve.wait_ge(S["out_mm"], j.n - 1)
                for odd in range(2):
                    first = 4 * r + odd
                    dve.wait_ge(S["ga_mm"], HEADS * j.n + first + 3)
                    dve.tensor_tensor(amat[j.par][:, first:first + 3:2, :],
                                      PS[:, 2 * odd + r % 2, :].rearrange("p (i m t) -> p i m t", i=2, m=2)[:, :, 1, :],
                                      mask_a.unsqueeze(1).to_broadcast([P, 2, P]), ALU.mult).then_inc(S["at_ready"], 1)

            def take_n(j, r):
                if r == 0 and j.after(1):
                    dve.wait_ge(S["n_stored"], 16 * NBLK * j.n)
                    dve.wait_ge(S["f_mm"], 3 * j.n)
                for odd in range(2):
                    dve.wait_ge(S["ga_mm"], HEADS * j.n + 4 * r + 3 + odd)
                    for i in range(2):
                        h = 4 * r + odd + 2 * i
                        dve.scalar_tensor_tensor(out=nmat[:, h, :], in0=PS[:, 2 * odd + r % 2, 256 * i:256 * i + P],
                                                 scalar=norm[:, 5, h:h + 1], in1=mask_n, op0=ALU.mult, op1=ALU.mult)\
                           .then_inc(S["n_ready"], 1)

            def take_norm(j):
                dve.wait_ge(S["norm_mm"], j.n + 1)
                dve.tensor_copy(norm[:, 0, :], PS[:, 3, 0:HEADS]).then_inc(S["norm_copied"], 1)

            def inverse_norms(j):
                dve.wait_ge(S["n1"], j.n + 1)
                dve.tensor_scalar(norm[:, 2, :], norm[:, 1, :], 1e-6, None, ALU.add).then_inc(S["n2"], 1)
                dve.wait_ge(S["n2"], j.n + 1)
                dve.reciprocal(norm[:, 3, :], norm[:, 2, :]).then_inc(S["n3"], 1)
                dve.wait_ge(S["n3"], j.n + 1)
                dve.tensor_tensor(norm[:, 4, :], norm[:, 3, :], norm[:, 3, :], ALU.mult).then_inc(S["n4"], 1)
                dve.wait_ge(S["n4"], j.n + 1)
                dve.wait_ge(S["beta_ready"], 1)
                dve.tensor_tensor(norm[:, 5, :], norm[:, 4, :], beta_h[:, :], ALU.mult).then_inc(S["rn_ready"], 1)
                dve.wait_ge(S["rn_ready"], j.n + 1)

            def right_side(j):
                dve.wait_ge(S["vb_ready"], j.n + 1)
                dve.tensor_tensor(rhs[j.par].rearrange("p (g d) -> p g d", d=HD), vb.rearrange("p (g d) -> p g d", d=HD),
                                  norm[:, 3, :].unsqueeze(2).to_broadcast([P, HEADS, HD]), ALU.mult).then_inc(S["rscale_ready"], 1)

            def moments_h(t):
                dve.wait_ge(S[f"hp_in{t.par}"], (t.half + 1) * 16)
                dve.bn_stats(cstat[:, :], hp[t.par][:, :]).then_inc(S["cstat_ready"], 1)
                dve.wait_ge(S["cstat_ready"], t.n + 1)
                if t.after(1):
                    dve.wait_ge(S["c4"], t.n)
                settled(dve)
                dve.bn_aggr(cvar[:, :], cstat[:, :]).then_inc(S["cvar_ready"], 1)

            def normalise(t):
                dve.wait_ge(S["cvar_ready"], t.n + 1)
                dve.wait_ge(S["c2"], t.n + 1)
                if t.after(1):
                    dve.wait_ge(S["xT_mm"], t.n)
                dve.tensor_scalar(xn[:, :], hp[t.par][:, :], cvar[:, 0:1], rstd_parts[:, 1:2], ALU.subtract, ALU.mult)\
                   .then_inc(S["x_ready"], 1)
                dve.wait_ge(S["x_ready"], t.n + 1)
                dve.wait_ge(S["crstd_ready"], t.n + 1)
                dve.tensor_scalar(xh[:, :], xn[:, :], rstd_parts[:, 5:6], None, ALU.mult).then_inc(S["xh_ready"], 1)

            def split(t):
                dve.wait_ge(S["mod_ready"], 3 * t.n + 3)
                dve.wait_ge(S["xlin_copied"], 2 * t.n + 2)
                if t.after(1):
                    dve.wait_ge(S["proj3_mm"], 5 * t.n)
                dve.tensor_copy(xr_hi[:, :, :], x_aug[:, :, :]).then_inc(S["xr_hi"], 1)
                dve.wait_ge(S["xr_hi"], t.n + 1)
                dve.tensor_tensor(xr_lo[:, :, :], x_aug[:, :, :], xr_hi[:, :, :].bitcast(F32), ALU.subtract).then_inc(S["xr_ready"], 1)

            def moments_f(k):
                dve.wait_ge(S["f2_mm"], k.n + 1)
                dve.tensor_tensor(f2[:, :], PS[:, 7, 0:ATT], ffn_bias[:, :], ALU.add).then_inc(S["f2_read"], 1)
                dve.wait_ge(S["f2_read"], k.n + 1)
                dve.bn_stats(fstat[:, :], f2[:, :]).then_inc(S["fstat_ready"], 1)
                dve.wait_ge(S["fstat_ready"], k.n + 1)
                settled(dve)
                dve.bn_aggr(fvar[:, :], fstat[:, :]).then_inc(S["fvar_ready"], 1)

            def result(k):
                dve.wait_ge(S["fvar_ready"], k.n + 1)
                dve.wait_ge(S["f_rstd"], k.n + 1)
                dve.tensor_scalar(fhat[:, :], f2[:, :], fvar[:, 0:1], tr[:, 3:4], ALU.subtract, ALU.mult).then_inc(S["fhat_ready"], 1)
                dve.wait_ge(S["fhat_ready"], k.n + 1)
                dve.tensor_tensor(fg[:, :], fhat[:, :], gamma[:, :], ALU.mult).then_inc(S["fg_ready"], 1)
                dve.wait_ge(S["fg_ready"], k.n + 1)
                dve.tensor_tensor(fb[:, :], fg[:, :], h2[:, :], ALU.add).then_inc(S["fb_ready"], 1)
                dve.wait_ge(S["fb_ready"], k.n + 1)
                if k.after(2):
                    dve.wait_ge(S[f"out{k.par}"], k.half * 16)
                dve.tensor_tensor(res[k.par][:, :], fb[:, :], beta[:, :], ALU.add).then_inc(S["res_ready"], 1)

            def step_c(it, u):
                t, j, k = Step(it, u), Step(it, u, 1), Step(it, u, 2)
                new, mid, old = t.inside(TILES), j.inside(TILES), k.inside(TILES)
                if new:
                    moments_h(t)
                    normalise(t)
                if mid:
                    take_norm(j)
                    shift_v(j)
                    take_a(j, 0)
                    take_a(j, 1)
                    inverse_norms(j)
                if old:
                    take_e(k)
                if mid:
                    take_n(j, 0)
                    take_n(j, 1)
                if old:
                    take_c(k, 0)
                if mid:
                    take_n(j, 2)
                    take_a(j, 2)
                if new:
                    split(t)
                if old:
                    take_c(k, 1)
                if mid:
                    right_side(j)
                if new:
                    moments(t, 0)
                if mid:
                    invert(j, range(1, 4))
                if old:
                    take_c(k, 2)
                if new:
                    moments(t, 1)
                if mid:
                    invert(j, range(4, 9))
                if old:
                    gate_and_add(k)
                if new:
                    scale_kq(t)
                if old:
                    norm_h2(k)
                if new:
                    scale_v(t)
                if mid:
                    invert(j, range(9, 13))
                if old:
                    moments_f(k)
                if mid:
                    invert(j, range(13, BLK))
                if old:
                    result(k)

            pipeline(dve, TILES, 2, step_c)


def host_layout(i):
    import numpy as np
    a = {k.replace("L0_", ""): np.asarray(v) for k, v in i.items()}
    row = lambda x: x.reshape(1, -1)
    flat = a["x"].reshape(BATCH, 3, 8, 16, 8, 16).transpose(0, 2, 4, 1, 3, 5).reshape(BATCH, NPATCH, INF)
    d = {}
    d["x"] = flat.transpose(1, 2, 0).reshape(PAIRS, 2, P, CH, BATCH).transpose(0, 2, 3, 1, 4).reshape(PAIRS, P, CH, P)
    for w in ("Wq", "Wk", "Wv"):
        d[w] = a["tok_" + w].reshape(PAIRS, 2, P, CH, ATT)
    halves = lambda b: b.reshape(PAIRS, 2, 2, HALF)
    d["bqk"] = np.concatenate([halves(a["tok_bq"]), halves(a["tok_bk"])], axis=2).transpose(0, 3, 1, 2)
    d["bv"] = a["tok_bv"].reshape(PAIRS, 2, 1, ATT)
    d["p1_w"] = a["tok_p1_w"].reshape(P, CH, ATT)
    chunked = lambda w: w.reshape(HC, P, -1).transpose(1, 0, 2)
    d["w0T"] = chunked(np.concatenate([a["tok_w0"].T, a["tok_b0"].reshape(-1, 1)], axis=1))
    for w in ("w1", "w2", "w3", "w4"):
        d[w] = chunked(a["tok_" + w])
    d["chain_b"] = np.stack([a["tok_" + b].reshape(HC, P).T for b in ("b1", "b2", "b3")], axis=1)
    d["p2"] = np.concatenate([a["tok_p2_w"], row(a["tok_p2_b"])])
    d["b4"] = row(a["tok_b4"])
    d["att_bias"] = np.concatenate([a["tok_ln_b"].reshape(2, HALF).T, a["tok_p1_b"].reshape(2, HALF).T], axis=1)
    d["tok_g"] = row(a["tok_ln_g"])
    twice = lambda b: np.concatenate([b, b])
    d["vecs"] = np.stack([a["attn_ln_in_g"][0:P], a["attn_ln_in_g"][0:P], a["attn_ln_in_b"][0:P], a["attn_ln_in_b"][0:P],
                          twice(a["attn_lnk_g"]), twice(a["attn_lnk_b"]), twice(a["attn_lnq_g"]), twice(a["attn_lnq_b"]),
                          a["ffn_b1"]], axis=1)
    d["vecs2"] = np.stack([a["attn_ln_in_g"][P:], a["attn_ln_in_b"][P:]], axis=1)
    d["mod_bias"] = np.stack([a[f"attn_{m}m_b1"] for m in "kqv"], axis=1)
    d["mod1T"] = np.concatenate([a[f"attn_{m}m_w1"].T for m in "kqv"], axis=1)
    d["modT"] = np.concatenate([np.concatenate([a[f"attn_{m}m_w2"].T, row(a[f"attn_{m}m_b2"])]) for m in "kqv"], axis=1)
    d["kqvT"] = np.concatenate([a["attn_Wk"].T, a["attn_Wq"].T, a["attn_Wv"].T], axis=1)
    d["gateT"] = np.concatenate([a["attn_Wg"].T, row(a["attn_bg"])])
    d["WoT"] = a["attn_Wo"].T.reshape(HEADS // 2, P, ATT).transpose(1, 0, 2)
    d["lnv_g"], d["lnv_b"] = row(a["attn_lnv_g"]), row(a["attn_lnv_b"])
    d["lr_scale"] = row(a["attn_lr_scale"])
    d["ffn1T"] = a["ffn_W1"].T
    d["ffn_w2"] = a["ffn_W2"].reshape(2, HALF, INNER).transpose(1, 0, 2)
    d["ffn_wo"] = a["ffn_Wo"].T.reshape(2, HALF, ATT).transpose(1, 0, 2)
    d["ffn_b2"] = a["ffn_b2"].reshape(2, HALF).T
    d["bo"], d["gamma"], d["beta"] = row(a["ffn_bo"]), row(a["ffn_gamma"]), row(a["ffn_beta"])
    n = np.arange(P)
    same = n[:, None] // 64 == n[None, :] // 64
    below, above = (n[:, None] > n[None, :]) & same, (n[:, None] < n[None, :]) & same
    outside = n[:, None] // BLK != n[None, :] // BLK
    heads = n[:, None] // HD == np.arange(2)[None, :]
    d["consts"] = np.concatenate([np.eye(P), -1.0 * below, above, above & outside, heads], axis=1).astype(np.float32)
    return {k: np.ascontiguousarray(v) for k, v in d.items()}


def kernel(**inputs):
    import numpy as np
    import concourse.bacc as bacc
    from concourse.bass_utils import run_bass_kernel_spmd as run
    nc = bacc.Bacc("TRN2", target_bir_lowering=False, num_devices=1)
    arrays = {"in_" + k: v for k, v in host_layout(inputs).items()}
    d = {k[3:]: nc.dram_tensor(k, v.shape, mybir.dt.from_np(v.dtype), kind="ExternalInput").ap() for k, v in arrays.items()}
    out = nc.dram_tensor("out", (BATCH, NPATCH, ATT), F32, kind="ExternalOutput").ap()
    build(nc, d, out)
    return run(nc, [arrays], core_ids=[0]).results[0]["out"]
```
